# Optimizing a Trainium2 kernel written in Bass

```python
import numpy as np
import jax
import jax.numpy as jnp

def _softmax(x, axis=-1):
    return jax.nn.softmax(x, axis=axis)

def _gelu(x):
    return jax.nn.gelu(x, approximate=True)

def _silu(x):
    return jax.nn.silu(x)

def _sigmoid(x):
    return jax.nn.sigmoid(x)

def _layernorm(x, axis=-1, eps=1e-05):
    m = jnp.mean(x, axis=axis, keepdims=True)
    v = jnp.var(x, axis=axis, keepdims=True)
    return (x - m) / jnp.sqrt(v + eps)

def _scatter_add(tgt, idx, src, axis=0):
    return tgt.at[idx].add(src)

def _segment_sum(src, seg, n):
    return jax.ops.segment_sum(src, seg, n)
kernel_name = 'mk_hybrid_d1_jaxref_r8_11f4c0'

def setup_inputs(seed: int=0):
    np.random.seed(seed)
    _w = jnp.asarray

    def _L0_attn_a_setup():
        import jax, jax.numpy as jnp
        import numpy as np
        EPS = 1e-05

        def _layernorm(x, gamma, beta):
            m = jnp.mean(x, axis=-1, keepdims=True)
            v = jnp.mean(jnp.square(x - m), axis=-1, keepdims=True)
            return (x - m) * jax.lax.rsqrt(v + EPS) * gamma + beta
        key = jax.random.key(seed)
        B, Q, C, H = (4, 512, 128, 16)
        hd = C // H
        ks = jax.random.split(key, 8)
        s_in = 1.0 / np.sqrt(C)
        return {'x': jax.random.normal(ks[0], (B, Q, C), jnp.float32), 'qkv_w': jax.random.normal(ks[1], (3 * C, C), jnp.float32) * s_in, 'qkv_b': jnp.zeros((3 * C,), jnp.float32), 'kn_g': jnp.ones((hd,), jnp.float32), 'kn_b': jnp.zeros((hd,), jnp.float32), 'vn_g': jnp.ones((hd,), jnp.float32), 'vn_b': jnp.zeros((hd,), jnp.float32), 'temperature': jnp.ones((H, 1, 1), jnp.float32), 'attn_bias': jnp.zeros((H, hd, hd), jnp.float32), 'p1_w': jax.random.normal(ks[2], (C, C), jnp.float32) * s_in, 'p1_b': jnp.zeros((C,), jnp.float32), 'p2_w': jax.random.normal(ks[3], (C, C), jnp.float32) * s_in, 'p2_b': jnp.zeros((C,), jnp.float32)}
    _L0_attn_a_in = _L0_attn_a_setup()

    def _L0_attn_b_setup():
        import jax, jax.numpy as jnp
        import numpy as np
        B, N, D = (2, 256, 128)
        H, DH = (16, 64)
        key = jax.random.key(seed)
        ks = jax.random.split(key, 5)
        s = 0.02
        return {'x': jax.random.normal(ks[0], (B, N, D), dtype=jnp.float32), 'W_w': jax.random.normal(ks[1], (3 * H * DH, D), dtype=jnp.float32) * s, 'W_b': jax.random.normal(ks[2], (3 * H * DH,), dtype=jnp.float32) * s, 'out_w': jax.random.normal(ks[3], (D, H * DH), dtype=jnp.float32) * s, 'out_b': jax.random.normal(ks[4], (D,), dtype=jnp.float32) * s}
    _L0_attn_b_in = _L0_attn_b_setup()

    def _L0_ffn_setup():
        import jax, jax.numpy as jnp
        import numpy as np
        DIM = 128
        HIDDEN = 384
        SCALE = 1.0 / 127.0

        def _dequant(w_int, dtype):
            return w_int.astype(dtype) * jnp.asarray(SCALE, dtype)
        key = jax.random.key(seed)
        k_x, k_g, k_u, k_d = jax.random.split(key, 4)
        x = jax.random.normal(k_x, (4, 256, DIM), dtype=jnp.float32)
        w_gate = jax.random.randint(k_g, (HIDDEN, DIM), -127, 128, dtype=jnp.int32)
        w_up = jax.random.randint(k_u, (HIDDEN, DIM), -127, 128, dtype=jnp.int32)
        w_down = jax.random.randint(k_d, (DIM, HIDDEN), -127, 128, dtype=jnp.int32)
        return {'x': x, 'w_gate': w_gate, 'w_up': w_up, 'w_down': w_down}
    _L0_ffn_in = _L0_ffn_setup()
    _d = {'L0_attn_a_x': _L0_attn_a_in['x'], 'L0_attn_a_qkv_w': _L0_attn_a_in['qkv_w'], 'L0_attn_a_qkv_b': _L0_attn_a_in['qkv_b'], 'L0_attn_a_kn_g': _L0_attn_a_in['kn_g'], 'L0_attn_a_kn_b': _L0_attn_a_in['kn_b'], 'L0_attn_a_vn_g': _L0_attn_a_in['vn_g'], 'L0_attn_a_vn_b': _L0_attn_a_in['vn_b'], 'L0_attn_a_temperature': _L0_attn_a_in['temperature'], 'L0_attn_a_attn_bias': _L0_attn_a_in['attn_bias'], 'L0_attn_a_p1_w': _L0_attn_a_in['p1_w'], 'L0_attn_a_p1_b': _L0_attn_a_in['p1_b'], 'L0_attn_a_p2_w': _L0_attn_a_in['p2_w'], 'L0_attn_a_p2_b': _L0_attn_a_in['p2_b'], 'L0_attn_b_W_w': _L0_attn_b_in['W_w'], 'L0_attn_b_W_b': _L0_attn_b_in['W_b'], 'L0_attn_b_out_w': _L0_attn_b_in['out_w'], 'L0_attn_b_out_b': _L0_attn_b_in['out_b'], 'L0_ffn_w_gate': _L0_ffn_in['w_gate'], 'L0_ffn_w_up': _L0_ffn_in['w_up'], 'L0_ffn_w_down': _L0_ffn_in['w_down']}
    _x0 = _d['L0_attn_a_x']
    _d['L0_attn_a_x'] = jax.random.normal(jax.random.fold_in(jax.random.key(seed), 1), (1, 2048, 128), dtype=_x0.dtype)
    del _x0
    return _d

def reference(L0_attn_a_x, L0_attn_a_qkv_w, L0_attn_a_qkv_b, L0_attn_a_kn_g, L0_attn_a_kn_b, L0_attn_a_vn_g, L0_attn_a_vn_b, L0_attn_a_temperature, L0_attn_a_attn_bias, L0_attn_a_p1_w, L0_attn_a_p1_b, L0_attn_a_p2_w, L0_attn_a_p2_b, L0_attn_b_W_w, L0_attn_b_W_b, L0_attn_b_out_w, L0_attn_b_out_b, L0_ffn_w_gate, L0_ffn_w_up, L0_ffn_w_down):

    def _L0_attn_a_ref(x, qkv_w, qkv_b, kn_g, kn_b, vn_g, vn_b, temperature, attn_bias, p1_w, p1_b, p2_w, p2_b):
        import jax, jax.numpy as jnp
        import numpy as np
        EPS = 1e-05

        def _layernorm(x, gamma, beta):
            m = jnp.mean(x, axis=-1, keepdims=True)
            v = jnp.mean(jnp.square(x - m), axis=-1, keepdims=True)
            return (x - m) * jax.lax.rsqrt(v + EPS) * gamma + beta
        B, Q, C = x.shape
        H = temperature.shape[0]
        hd = C // H
        qkv = (x @ qkv_w.T + qkv_b).reshape(B, Q, 3, H, hd)
        qkv = jnp.transpose(qkv, (2, 0, 3, 1, 4))
        q, k, v = (qkv[0], qkv[1], qkv[2])
        k = _layernorm(k, kn_g, kn_b)
        v = _layernorm(v, vn_g, vn_b)
        kv = jnp.einsum('bhqd,bhqe->bhde', k, v) / Q * temperature + attn_bias
        att = jnp.einsum('bhqd,bhde->bhqe', q, kv)
        att = jnp.transpose(att, (0, 2, 1, 3)).reshape(B, Q, C) + x
        h = jax.nn.gelu(att @ p1_w.T + p1_b, approximate=False)
        return h @ p2_w.T + p2_b + x

    def _L0_attn_b_ref(x, W_w, W_b, out_w, out_b):
        import jax, jax.numpy as jnp
        import numpy as np
        B, N, D = (2, 256, 128)
        H, DH = (16, 64)
        b, n, _ = x.shape
        qkv = x @ W_w.T + W_b
        Q, K, V = jnp.split(qkv, 3, axis=-1)
        split_heads = lambda t: t.reshape(b, n, H, DH).transpose(0, 2, 1, 3)
        q, k, v = map(split_heads, (Q, K, V))
        scale = DH ** (-0.5)
        dots = jnp.einsum('bhik,bhjk->bhij', q, k) * scale
        attn = jax.nn.softmax(dots, axis=-1)
        out = jnp.einsum('bhij,bhjk->bhik', attn, v)
        out = out.transpose(0, 2, 1, 3).reshape(b, n, H * DH)
        return out @ out_w.T + out_b

    def _L0_ffn_ref(x, w_gate, w_up, w_down):
        import jax, jax.numpy as jnp
        import numpy as np
        DIM = 128
        HIDDEN = 384
        SCALE = 1.0 / 127.0

        def _dequant(w_int, dtype):
            return w_int.astype(dtype) * jnp.asarray(SCALE, dtype)
        wg = _dequant(w_gate, x.dtype)
        wu = _dequant(w_up, x.dtype)
        wd = _dequant(w_down, x.dtype)
        gate = jnp.einsum('bsd,hd->bsh', x, wg)
        up = jnp.einsum('bsd,hd->bsh', x, wu)
        h = jax.nn.silu(gate) * up
        return jnp.einsum('bsh,dh->bsd', h, wd)
    x = L0_attn_a_x
    x = x + _L0_attn_a_ref(_layernorm(x, axis=-1), L0_attn_a_qkv_w, L0_attn_a_qkv_b, L0_attn_a_kn_g, L0_attn_a_kn_b, L0_attn_a_vn_g, L0_attn_a_vn_b, L0_attn_a_temperature, L0_attn_a_attn_bias, L0_attn_a_p1_w, L0_attn_a_p1_b, L0_attn_a_p2_w, L0_attn_a_p2_b)
    x = x + _L0_ffn_ref(_layernorm(x, axis=-1), L0_ffn_w_gate, L0_ffn_w_up, L0_ffn_w_down)
    x = x + _L0_attn_b_ref(_layernorm(x, axis=-1), L0_attn_b_W_w, L0_attn_b_W_b, L0_attn_b_out_w, L0_attn_b_out_b)
    x = x + _L0_ffn_ref(_layernorm(x, axis=-1), L0_ffn_w_gate, L0_ffn_w_up, L0_ffn_w_down)
    return x

_drawn_inputs = setup_inputs


def setup_inputs(seed=0):
    import zlib

    import numpy as np

    out = dict(_drawn_inputs(seed))
    spreads = {'L0_attn_a_qkv_b': (0.0, 0.1),
     'L0_attn_a_kn_g': (1.0, 0.6),
     'L0_attn_a_kn_b': (0.0, 0.467),
     'L0_attn_a_vn_g': (1.0, 0.6),
     'L0_attn_a_vn_b': (0.0, 0.532),
     'L0_attn_a_temperature': (1.0, 0.578),
     'L0_attn_a_attn_bias': (0.0, 0.1),
     'L0_attn_a_p1_b': (0.0, 0.1),
     'L0_attn_a_p2_b': (0.0, 0.1)}
    factors = {'L0_attn_b_W_w': 30.747,
     'L0_attn_b_W_b': 64.0,
     'L0_attn_b_out_w': 30.664,
     'L0_attn_b_out_b': 64.0}
    for name, (base, spread) in spreads.items():
        noise = np.random.default_rng([zlib.crc32(name.encode()), seed]).standard_normal(out[name].shape)
        drawn = base * np.exp(spread * noise) if base else spread * noise
        out[name] = jnp.asarray(drawn.astype(out[name].dtype))
    for name, factor in factors.items():
        out[name] = (out[name] * factor).astype(out[name].dtype)
    return out
```

```python
import math
from contextlib import ExitStack

import concourse.bass as bass
from concourse import mybir

F32 = mybir.dt.float32
F32R = mybir.dt.float32r
F16 = mybir.dt.float16
I32 = mybir.dt.int32
ALU = mybir.AluOpType
ACT = mybir.ActivationFunctionType
AX = mybir.AxisListType.X

P = 128
EPS = 1e-5
BLK = 512
DH = 64
HD = 8
VW = 2 * DH + 1
LAG = 3
RING = 4
P_SCALE = math.log(32.0)
V_LIMIT = 2.0 ** 13

PAIR = 64
HEAD = 32
ROT = 6
MAX_FROM = 5
SIDE = 3
SHIFT_AT = 29


def aux_jobs(p, last):
    v, parity = p % HEAD, (p // HEAD + 1) % 2
    jobs = []
    for b in range(4):
        if p % PAIR == (HEAD + 8 * b + 12) % PAIR:
            jobs.append(("turn", b))
        if p % PAIR == (HEAD + 8 * b + 13) % PAIR:
            jobs.append(("out", b))
    if last and p >= HEAD:
        return jobs
    if v < 2:
        jobs += [("proj", parity, 2 * v), ("proj", parity, 2 * v + 1)]
    if MAX_FROM <= v < SHIFT_AT:
        n = sum(SIDE - len(aux_jobs(p - v + u + PAIR, True)) for u in range(MAX_FROM, v))
        jobs += [("max", parity, k) for k in range(n, min(64, n + SIDE - len(jobs)))]
    if v == SHIFT_AT:
        jobs.append(("shift", parity))
    return jobs


def max_operands(n):
    return (n // 2, n % 2) if n < 16 else (8 + (n - 16) // 2, n % 2) if n < 32 else ((n - 32) // 2, 2 + n % 2)


def low_on_dve(p, last):
    if last and HEAD <= p:
        return p % 3 == 1
    return p % HEAD in (3, 30)


def block_program(nc, a):
    T = a["xT"].shape[1]
    C = P
    NT, NB = T // P, T // BLK
    H2 = a["wkq"].shape[0]
    NP = H2 // 2
    FH = a["wd"].shape[0] // P
    assert T == 2048 and a["xT"].shape[0] == C and H2 * DH == 1024 and FH == 3

    with ExitStack() as ctx:
        def sb(name, shape, dt=F32):
            return ctx.enter_context(nc.sbuf_tensor(name, shape, dt))

        def sem(name):
            return ctx.enter_context(nc.semaphore(name))

        ps = ctx.enter_context(nc.psum_tensor("ps", [P, 8, BLK], F32))
        s_ps = ps[:, 0:4, :].rearrange("p (r k) n -> p r k n", r=2)
        o_ps = ps[:, 4:6, :]
        aux_ps = ps[:, 6:8, :]

        xT = sb("xT_sb", [P, T])
        xnT = sb("xnT", [P, T])
        consts = sb("consts", [P, 3, P])
        ident, centre, mean = (consts[:, i, :] for i in range(3))
        eps = sb("eps", [P, 1])
        k1 = [sb(f"k1_{i}", [P, T], F32R) for i in range(2)]
        k2 = [sb(f"k2_{i}", [P, T], F32R) for i in range(2)]
        q1 = [sb(f"q1_{i}", [P, T], F32R) for i in range(2)]
        q2 = [sb(f"q2_{i}", [P, T], F32R) for i in range(2)]
        v_flat = sb("v_all", [P, H2 * NT * VW], F16)
        v_all = v_flat[:].rearrange("p (h t v) -> p h t v", h=H2, t=NT)
        v_head = [sb(f"v_head{i}", [P, NT, VW], F16) for i in range(2)]
        wkq = [sb(f"wkq{i}", [P, P]) for i in range(2)]
        bkq = [sb(f"bkq{i}", [P, 1]) for i in range(2)]
        wo = sb("wo_pair", [P, C])
        unscale = sb("unscale", [P, 1])
        p32 = sb("p32", [P, RING, 2 * BLK])
        p_hi = sb("p_hi", [P, RING, 2 * BLK], F16)
        p_lo = sb("p_lo", [P, RING, 2 * BLK], F16)
        maxes = sb("maxes", [P, NT, NB])
        row_max = sb("row_max", [P, NT])
        neg_max = sb("neg_max", [P, NT])
        shift = sb("shift", [NT, P], F32R)
        rden = sb("rden", [P, 2, 2])
        o_low = sb("o_low", [P, 2, 2, DH])
        o_sb = sb("o_sb", [P, NT, 2 * DH])
        oT = sb("oT", [P, BLK])
        v_unscale = sb("v_unscale", [P, NP])
        v_bias = sb("v_bias", [P, NP])
        out_b = sb("out_b", [P, 1])
        y_bias = sb("y_bias", [P, 1])
        v_norm = sb("v_norm", [P, NP])
        v_pow = sb("v_pow", [P, NP])
        v_scale = sb("v_scale", [P, NP])
        wgu = sb("wgu", [P, 2 * FH, P])
        wd = sb("wd", [P, FH, P])

        room = v_flat[:].bitcast(F32)
        at = [0]

        def carve(n):
            at[0] += n
            assert at[0] <= room.shape[1]
            return room[:, at[0] - n:at[0]]

        kv = carve(NT * 256).rearrange("p (t n) -> p t n", n=256)
        kv_sq = carve(2048).rearrange("p (r n) -> p r n", r=2)
        qT, attT, hT = carve(T), carve(T), carve(T)
        wkv = carve(512).rearrange("p (s n) -> p s n", s=2)
        wkv_mean = carve(64)
        wq, p1w, p2w, mask = (carve(P) for _ in range(4))
        gamma, beta = carve(256), carve(256)
        gb8 = carve(4 * HD).rearrange("p (s n) -> p s n", n=HD)
        kv_rstd = carve(4 * 128).rearrange("p (u n) -> p u n", u=4)
        kv_bias8 = carve(HD)
        kv_bd, kv_bias = carve(P), carve(P)
        bq, p1b, p2b, temp = (carve(1) for _ in range(4))
        ff_room = room[:, 0:6 * BLK + 2 * BLK]
        ff_h = ff_room[:, 0:6 * BLK].rearrange("p (r n) -> p r n", r=6)
        ff_s = ff_room[:, 6 * BLK:8 * BLK].rearrange("p (r n) -> p r n", r=2)
        wv = p_hi[:].rearrange("p r n -> p (r n)").bitcast(F32)[:, 0:1024].rearrange("p (j c) -> p j c", c=C)
        wv_sq = p_hi[:].rearrange("p r n -> p (r n)").bitcast(F32)[:, 1024:2048].rearrange("p (j c) -> p j c", c=C)
        ints = p_lo[:].rearrange("p r n -> p (r n)").bitcast(I32)[:, 0:3 * FH * P].rearrange("p (j c) -> p j c", c=P)
        wvT = o_sb[:].rearrange("p t n -> p (t n)")[:, 0:1024]
        woT = o_sb[:].rearrange("p t n -> p (t n)")[:, 1024:2048].rearrange("p (j c) -> p j c", c=C)
        ln_sq = p32[:, :, 0:BLK]
        ln_std = p32[:, :, BLK:2 * BLK]

        def f32(ap):
            return ap.bitcast(F32)

        x_in = [sem(f"x_in{b}") for b in range(NB)]
        const_in, a_in, ff_in, vw_in, bias_in = (
            sem(n) for n in ("const_in", "a_in", "ff_in", "vw_in", "bias_in"))
        dve_step = sem("dve_step")
        centred, squared, averaged, rooted, normed = (
            sem(n) for n in ("centred", "squared", "averaged", "rooted", "normed"))
        kv_done, kv_moved, kv_squared, kv_summed, kv_rooted, kv_scaled, kv_gamma, kv_ready = (
            sem(n) for n in ("kv_done", "kv_moved", "kv_squared", "kv_summed", "kv_rooted", "kv_scaled",
                             "kv_gamma", "kv_ready"))
        gamma_ready, q_done, q_moved, kvprod_done, kv_bd_ready = (
            sem(n) for n in ("gamma_ready", "q_done", "q_moved", "kvprod_done", "kv_bd_ready"))
        att_done, att_moved, p1_done, gelu_done, p2_done, x_new = (
            sem(n) for n in ("att_done", "att_moved", "p1_done", "gelu_done", "p2_done", "x_new"))
        ff_ready, gu_done, silu_done, h_done, down_done = (
            sem(n) for n in ("ff_ready", "gu_done", "silu_done", "h_done", "down_done"))
        v_summed, v_rooted, wv_scaled, wv_turned, wv_ready, v_done, v_hi_done, v_lo_done, ones_done = (
            sem(n) for n in ("v_summed", "v_rooted", "wv_scaled", "wv_turned", "wv_ready", "v_done",
                             "v_hi_done", "v_lo_done", "ones_done"))
        w_in = [sem(f"w_in{i}") for i in range(2)]
        v_in = [sem(f"v_in{i}") for i in range(2)]
        wo_in = sem("wo_in")
        kq_split = sem("kq_split")
        spread_hi = sem("spread_hi")
        spread_lo = [sem(f"spread_lo{i}") for i in range(2)]
        shift_ready, shift_in = sem("shift_ready"), sem("shift_in")
        neg_max_ready = sem("neg_max_ready")
        aux_done, aux_used = sem("aux_done"), sem("aux_used")
        scores_done, exp_done, hi_done = sem("scores_done"), sem("exp_done"), sem("hi_done")
        lo_pool, lo_dve = sem("lo_pool"), sem("lo_dve")
        pv_done, o_read, o_used = sem("pv_done"), sem("o_read"), sem("o_used")
        stored = sem("stored")

        AUX_PAIR = sum(len(aux_jobs(p, False)) for p in range(ROT, ROT + PAIR))
        def first_jobs(p):
            return [j for j in aux_jobs(p, False) if j[0] in ("proj", "max", "shift")]

        PROLOGUE = [j for p in range(ROT) for j in first_jobs(p)]
        AUX_FIRST = NB + 4 * NT + 1
        assert AUX_PAIR % 2 == 0

        def aux_before(p, last, first=False):
            if first:
                return AUX_FIRST + sum(len(first_jobs(q)) for q in range(p))
            return AUX_FIRST + len(PROLOGUE) + sum(len(aux_jobs(q, last)) for q in range(ROT, p))

        def low_count(p, last, dve):
            return sum(low_on_dve(q % PAIR, last) == dve for q in range(p + 1))

        LOW_PAIR = {dve: low_count(PAIR - 1, False, dve) for dve in (True, False)}

        block = ctx.enter_context(nc.Block())

        @block.sync
        def _(sp):
            for b in range(NB):
                sp.dma_start(xT[:, b * BLK:(b + 1) * BLK], a["xT"][:, b * BLK:(b + 1) * BLK]).then_inc(x_in[b], 16)
            sp.dma_start(wkv[:, 0, :], a["wqkvT"][:, C:3 * C]).then_inc(a_in, 16)
            sp.dma_start(wkv[:, 1, :], a["qkvb"][C:3 * C].rearrange("(o n) -> o n", o=1).broadcast_to([P, 2 * C])
                         ).then_inc(a_in, 16)
            sp.dma_start(wq, a["wqkvT"][:, 0:C]).then_inc(a_in, 16)
            sp.dma_start(bq, a["qkvb"][0:C].rearrange("(n o) -> n o", o=1)).then_inc(a_in, 16)
            for i, name in enumerate(("kn_g", "vn_g", "kn_b", "vn_b")):
                sp.dma_start(gb8[:, i, :], a[name].rearrange("(o n) -> o n", o=1).broadcast_to([P, HD])
                             ).then_inc(a_in, 16)
            sp.dma_start(mask, a["mask"]).then_inc(a_in, 16)
            sp.dma_start(kv_bias8, a["attn_bias"].rearrange("h d e -> (h d) e")).then_inc(a_in, 16)
            for h in range(C // HD):
                sp.dma_start(temp[h * HD:(h + 1) * HD, :], a["temperature"][h:h + 1, 0, :].broadcast_to([HD, 1])
                             ).then_inc(a_in, 16)
            sp.dma_start(p1w, a["p1T"]).then_inc(a_in, 16)
            sp.dma_start(p2w, a["p2T"]).then_inc(a_in, 16)
            sp.dma_start(p1b, a["p1b"].rearrange("(n o) -> n o", o=1)).then_inc(a_in, 16)
            sp.dma_start(p2b, a["p2b"].rearrange("(n o) -> n o", o=1)).then_inc(a_in, 16)

            def load_w(i, n):
                sp.dma_start(wkq[i][:], a["wkq"][bass.ds(n, 1), :, :].rearrange("o c m -> (o c) m")
                             ).then_inc(w_in[i], 16)
                sp.dma_start(bkq[i][:], a["bkq"][bass.ds(n, 1), :].rearrange("o (m u) -> (o m) u", u=1)
                             ).then_inc(w_in[i], 16)

            def load_v(i, n):
                sp.dma_start(v_head[i][:].rearrange("p t v -> p (t v)"),
                             v_all[:, bass.ds(n, 1), :, :].rearrange("p o t v -> p (o t v)")).then_inc(v_in[i], 16)

            def load_wo(g):
                sp.dma_start(wo[:], a["woT"][bass.ds(g * P, P), :]).then_inc(wo_in, 16)
                sp.dma_start(unscale[:], v_unscale[:, bass.ds(g, 1)]).then_inc(wo_in, 16)

            def spread(i, n, half):
                cols = slice(half * T // 2, (half + 1) * T // 2)
                sp.wait_ge(kq_split, n * 2 + half + 1)
                sp.dma_start(f32(q1[i][0:DH, cols]), f32(k1[i][DH:P, cols])).then_inc(spread_hi, 16)
                sp.dma_start(f32(q1[i][DH:P, cols]), f32(k1[i][DH:P, cols])).then_inc(spread_hi, 16)
                sp.dma_start(f32(k2[i][DH:P, cols]), f32(k1[i][0:DH, cols])).then_inc(spread_hi, 16)
                sp.wait_ge(spread_hi, n * 96 + half * 48 + 48)
                sp.dma_start(f32(k1[i][DH:P, cols]), f32(q2[i][0:DH, cols])).then_inc(spread_lo[half], 16)

            def place_shift(i, n):
                sp.wait_ge(shift_ready, n + 1)
                for half in range(2):
                    sp.wait_ge(spread_lo[half], n * 16 + 16)
                sp.dma_start(f32(q2[i][0:1, :]).rearrange("o (t n) -> o t n", t=NT), f32(shift[:])).then_inc(shift_in, 16)

            load_w(0, 0)
            load_w(1, 1)
            for half in range(2):
                spread(0, 0, half)
            sp.wait_ge(v_lo_done, 2 * NT)
            sp.wait_ge(v_hi_done, 2 * NT)
            sp.wait_ge(ones_done, 1)
            load_v(0, 0)
            load_v(1, 1)
            load_wo(0)
            place_shift(0, 0)
            for half in range(2):
                spread(1, 1, half)

            def pair_moves(g, last):
                if not last:
                    load_w(0, g * 2 + 2)
                place_shift(1, g * 2 + 1)
                if last:
                    return
                for half in range(2):
                    spread(0, g * 2 + 2, half)
                load_w(1, g * 2 + 3)
                sp.wait_ge(pv_done, g * PAIR + HEAD)
                load_v(0, g * 2 + 2)
                place_shift(0, g * 2 + 2)
                for half in range(2):
                    spread(1, g * 2 + 3, half)
                sp.wait_ge(pv_done, g * PAIR + PAIR)
                load_v(1, g * 2 + 3)
                sp.wait_ge(aux_used, g * AUX_PAIR + aux_before(ROT + PAIR, False))
                load_wo(g + 1)

            with sp.Fori(0, NP - 1) as g:
                pair_moves(g, False)
            pair_moves(NP - 1, True)
            for b in range(NB):
                sp.wait_ge(x_new, 2 * NB + b + 1)
                sp.dma_start(a["out"][:, b * BLK:(b + 1) * BLK], xT[:, b * BLK:(b + 1) * BLK]).then_inc(stored, 16)
            sp.wait_ge(stored, 16 * NB)

        @block.tensor
        def _(pe):
            def cols(b):
                return slice(b * BLK, (b + 1) * BLK)

            def layernorm(k, x_ready):
                def average(b):
                    pe.wait_ge(squared, NB * k + b + 1)
                    pe.matmul(ps[:, 4 + b, :], mean, ln_sq[:, b, :], start=True, stop=True).then_inc(averaged, 1)

                for b in range(NB):
                    pe.wait_ge(*x_ready(b))
                    pe.matmul(ps[:, b, :], centre, xT[:, cols(b)], start=True, stop=True).then_inc(centred, 1)
                    if b:
                        average(b - 1)
                average(NB - 1)

            def swiglu(f, k):
                n = NB * FH

                def down(b):
                    pe.wait_ge(h_done, n * f + FH * (b + 1))
                    for j in range(FH):
                        last = pe.matmul(ps[:, b, :], wd[:, j, :], ff_h[:, (b % 2) * FH + j, :],
                                         start=(j == 0), stop=(j == FH - 1))
                    last.then_inc(down_done, 1)

                for i in range(n):
                    b, j = divmod(i, FH)
                    pe.wait_ge(normed, NB * k + (2 if i == 0 else NB))
                    if i >= 2:
                        pe.wait_ge(h_done, n * f + i - 1)
                    bank = 4 + 2 * (i % 2)
                    pe.matmul(ps[:, bank, :], wgu[:, j, :], xnT[:, cols(b)], start=True, stop=True)
                    pe.matmul(ps[:, bank + 1, :], wgu[:, FH + j, :], xnT[:, cols(b)], start=True, stop=True
                              ).then_inc(gu_done, 1)
                    if j == 1 and b:
                        down(b - 1)
                down(NB - 1)

            pe.wait_ge(const_in, 48)
            layernorm(0, lambda b: (x_in[b], 16))
            pe.wait_ge(gamma_ready, 1)
            for u in range(4):
                pe.wait_ge(normed, 2 if u == 0 else NB)
                for t in range(4 * u, 4 * u + 4):
                    last = pe.matmul(ps[:, t // 2, (t % 2) * 256:(t % 2) * 256 + 256], xnT[:, t * P:(t + 1) * P],
                                     wkv[:, 0, :], start=True, stop=True, skip_group_check=True)
                last.then_inc(kv_done, 1)
            for b in range(NB):
                pe.wait_ge(kv_moved, b // 2 + 1)
                pe.matmul(ps[:, b, :], wq, xnT[:, cols(b)], start=True, stop=True).then_inc(q_done, 1)
            pe.wait_ge(kv_moved, 4)
            pe.wait_ge(wv_scaled, 1)
            for j in range(NP):
                pe.transpose(ps[:, 5 + j // 4, (j % 4) * P:(j % 4 + 1) * P], wv[:, j, :], ident)
            pe.wait_ge(bias_in, 48)
            for j in range(NP):
                last = pe.matmul(ps[:, 7, 0:1], woT[:, j, :], v_bias[:, j:j + 1], start=(j == 0), stop=(j == NP - 1))
            last.then_inc(wv_turned, 1)
            for t in range(NT):
                pe.wait_ge(kv_ready, t // 4 + 1)
                last = pe.matmul(ps[:, 4, 0:P], kv[:, t, 0:P], kv[:, t, P:2 * P], start=(t == 0), stop=(t == NT - 1))
            last.then_inc(kvprod_done, 1)
            pe.wait_ge(kv_bd_ready, 1)
            pe.wait_ge(wv_ready, 1)
            for s in range(NB + 2):
                if s < NB:
                    pe.wait_ge(q_moved, s + 1)
                    pe.matmul(ps[:, s, :], kv_bd, qT[:, cols(s)], start=True, stop=True).then_inc(att_done, 1)
                if 1 <= s <= NB:
                    pe.wait_ge(att_moved, s)
                    pe.matmul(ps[:, 3 + s, :], p1w, attT[:, cols(s - 1)], start=True, stop=True).then_inc(p1_done, 1)
                if s >= 2:
                    pe.wait_ge(gelu_done, s - 1)
                    pe.matmul(ps[:, s - 2, :], p2w, hT[:, cols(s - 2)], start=True, stop=True).then_inc(p2_done, 1)

            layernorm(1, lambda b: (x_new, b + 1))
            pe.wait_ge(ff_ready, 1)
            swiglu(0, 1)
            layernorm(2, lambda b: (x_new, NB + b + 1))

            def aux(job, bank):
                out = aux_ps[:, bank, :]
                kind, i = job[0], job[1]
                if kind == "proj":
                    return pe.matmul(out, wkq[i][:], xnT[:, cols(job[2])], start=True, stop=True)
                if kind == "max":
                    t, kb = max_operands(job[2])
                    return pe.matmul(out, q1[i][:, t * P:(t + 1) * P], k1[i][:, cols(kb)], start=True, stop=True)
                if kind == "shift":
                    return pe.transpose(out[0:NT, 0:P], neg_max[:], ident)
                if kind == "turn":
                    for t in range(4):
                        last = pe.transpose(out[:, t * P:(t + 1) * P], o_sb[:, 4 * i + t, :], ident)
                    return last
                return pe.matmul(out, wo[:], oT[:], start=True, stop=True)

            def scores(p, kt):
                i, (qb, kp) = p // HEAD % 2, divmod(p % HEAD, 8)
                k = slice((2 * kp + kt) * P, (2 * kp + kt + 1) * P)
                out = s_ps[:, p % 2, kt, :]
                pe.matmul(out, k1[i][:, k], q1[i][:, cols(qb)], start=True, stop=False)
                last = pe.matmul(out, k2[i][:, k], q2[i][:, cols(qb)], start=False, stop=True)
                if kt == 1:
                    last.then_inc(scores_done, 1)

            def times_v(p):
                i, v = p // HEAD % 2, p % HEAD
                for kt in range(2):
                    k = 2 * (v % 8) + kt
                    for t in range(4):
                        at0 = (t % 2) * VW
                        w = slice(kt * BLK + t * P, kt * BLK + (t + 1) * P)
                        pe.matmul(o_ps[:, t // 2, at0:at0 + VW], p_hi[:, p % RING, w], v_head[i][:, k, :],
                                  start=(k == 0 and t % 2 == 0), stop=False, skip_group_check=True)
                        last = pe.matmul(o_ps[:, t // 2, at0:at0 + DH + 1], p_lo[:, p % RING, w],
                                         v_head[i][:, k, 0:DH + 1], start=False, stop=(k == NT - 1),
                                         skip_group_check=True)
                last.then_inc(pv_done, 1)

            pe.wait_ge(normed, 3 * NB)
            pe.wait_ge(w_in[0], 32)
            for b in range(NB):
                if b >= 2:
                    pe.wait_ge(aux_used, b - 1)
                aux(("proj", 0, b), b % 2).then_inc(aux_done, 1)

            def first_max(n):
                if n == 0:
                    pe.wait_ge(spread_lo[0], 16)
                if n == 16:
                    pe.wait_ge(spread_lo[1], 16)
                pe.wait_ge(aux_used, NB + n - 1)
                aux(("max", 0, n), n % 2).then_inc(aux_done, 1)

            AHEAD = 8
            for i in range(2 * NT):
                t, half = divmod(i, 2)
                if i >= 4:
                    pe.wait_ge(v_lo_done, i - 3)
                pe.matmul(ps[:, i % 4, :], xnT[:, t * P:(t + 1) * P], wvT[:, half * BLK:(half + 1) * BLK],
                          start=True, stop=True).then_inc(v_done, 1)
                if i >= AHEAD:
                    first_max(2 * (i - AHEAD))
                    first_max(2 * (i - AHEAD) + 1)
            for n in range(2 * (2 * NT - AHEAD), 4 * NT):
                first_max(n)
            pe.wait_ge(neg_max_ready, 1)
            pe.wait_ge(aux_used, NB + 4 * NT - 1)
            aux(("shift", 0), (NB + 4 * NT) % 2).then_inc(aux_done, 1)

            def tick(g, p, last, first=False):
                c = g * PAIR + p
                n = g * 2 + p // HEAD
                jobs = first_jobs(p) if first else aux_jobs(p, last)
                done = aux_before(p, last, first)

                def side(k):
                    if k >= len(jobs):
                        return
                    job, m = jobs[k], done + k if first else g * AUX_PAIR + done + k
                    if job[0] == "proj" and job[2] == 0:
                        pe.wait_ge(w_in[job[1]], (g + (p // HEAD + 1) // 2) * 32 + 32)
                    for half in range(2):
                        if job[0] == "max" and job[2] == 16 * half:
                            pe.wait_ge(spread_lo[half], (n + 1) * 16 + 16)
                    if job[0] == "shift":
                        pe.wait_ge(neg_max_ready, n + 2)
                    if job[0] == "turn":
                        pe.wait_ge(o_used, g * 8 + 5 + job[1])
                    if job[0] == "out" and job[1] == 0:
                        pe.wait_ge(wo_in, g * 32 + 32)
                    pe.wait_ge(aux_used, m if job[0] == "out" else m - 1)
                    aux(job, (done + k) % 2).then_inc(aux_done, 1)

                side(0)
                if not (last and p >= PAIR):
                    if p % HEAD == 0:
                        pe.wait_ge(shift_in, n * 16 + 16)
                    if first and p < 2:
                        pe.wait_ge(v_lo_done, 2 * NT)
                    else:
                        pe.wait_ge(hi_done, c - 1)
                    scores(p, 0)
                    side(1)
                    scores(p, 1)
                else:
                    side(1)
                side(2)
                q = p - LAG
                with_v = not (first and q < 0) and not (last and q >= PAIR)
                if with_v:
                    if q % HEAD == 0:
                        pe.wait_ge(v_in[q // HEAD % 2], (g + q // PAIR) * 16 + 16)
                    if q % 8 == 0 and not (first and q == 0):
                        pe.wait_ge(o_read, g * 8 + q // 8)
                    owner = low_on_dve(q % PAIR, last)
                    pe.wait_ge(lo_dve if owner else lo_pool, g * LOW_PAIR[owner] + low_count(q, last, owner))
                    times_v(q)
                assert len(jobs) <= 3

            for p in range(ROT):
                tick(0, p, False, first=True)
            with pe.Fori(0, NP - 1) as g:
                for p in range(ROT, ROT + PAIR):
                    tick(g, p, False)
            for p in range(ROT, ROT + PAIR):
                tick(NP - 1, p, True)

            layernorm(3, lambda b: (aux_used, (NP - 1) * AUX_PAIR + aux_before(ROT + PAIR, True)))
            swiglu(1, 3)

        @block.scalar
        def _(act):
            for i, name in enumerate(("ident", "centre", "mean")):
                act.dma_start(consts[:, i, :], a[name]).then_inc(const_in, 16)
            act.dma_start(wv, a["wv"].rearrange("(j p) c -> p j c", p=P)).then_inc(vw_in, 16)
            act.dma_start(ints[:, 0:FH, :], a["wg"].rearrange("c (j m) -> c j m", j=FH)).then_inc(ff_in, 16)
            act.dma_start(ints[:, FH:2 * FH, :], a["wu"].rearrange("c (j m) -> c j m", j=FH)).then_inc(ff_in, 16)
            act.dma_start(ints[:, 2 * FH:3 * FH, :], a["wd"].rearrange("(j p) d -> p j d", p=P)).then_inc(ff_in, 16)
            act.dma_start(woT, a["woT"].rearrange("(j p) d -> p j d", p=P)).then_inc(bias_in, 16)
            act.dma_start(v_bias[:], a["bv"]).then_inc(bias_in, 16)
            act.dma_start(out_b[:], a["outb"].rearrange("(n o) -> n o", o=1)).then_inc(bias_in, 16)

            def cols(b):
                return slice(b * BLK, (b + 1) * BLK)

            def layernorm(k):
                def root(b):
                    act.wait_ge(averaged, NB * k + b + 1)
                    nc.scalar.activation(ln_std[:, b, :], ps[:, 4 + b, :], ACT.Sqrt, bias=eps[:]).then_inc(rooted, 1)

                if k == 0:
                    act.wait_ge(ff_ready, 1)
                for b in range(NB):
                    act.wait_ge(centred, NB * k + b + 1)
                    nc.scalar.activation(ln_sq[:, b, :], ps[:, b, :], ACT.Square).then_inc(squared, 1)
                    if b:
                        root(b - 1)
                root(NB - 1)

            def swiglu(f):
                n = NB * FH
                for i in range(n):
                    act.wait_ge(gu_done, n * f + i + 1)
                    if i >= 2:
                        act.wait_ge(h_done, n * f + i - 1)
                    nc.scalar.activation(ff_s[:, i % 2, :], ps[:, 4 + 2 * (i % 2), :], ACT.Silu).then_inc(silu_done, 1)

            act.wait_ge(v_summed, 1)
            nc.scalar.activation(v_norm[:], v_norm[:], ACT.Sqrt, scale=float(C)).then_inc(v_rooted, 1)

            layernorm(0)
            for u in range(4):
                act.wait_ge(kv_moved, u + 1)
                if u >= 2:
                    act.wait_ge(kv_summed, u - 1)
                nc.scalar.activation(kv_sq[:, u % 2, :], kv[:, 4 * u:4 * u + 4, :].rearrange("p t n -> p (t n)"),
                                     ACT.Square).then_inc(kv_squared, 1)
                act.wait_ge(q_done, u + 1)
                nc.scalar.activation(qT[:, cols(u)], ps[:, u, :], ACT.Identity, bias=bq).then_inc(q_moved, 1)
                act.wait_ge(kv_summed, u + 1)
                nc.scalar.activation(kv_rstd[:, u, :], kv_rstd[:, u, :], ACT.Sqrt, bias=eps[:], scale=1.0 / HD
                                     ).then_inc(kv_rooted, 1)
            for b in range(NB):
                act.wait_ge(p1_done, b + 1)
                nc.scalar.activation(hT[:, cols(b)], ps[:, 4 + b, :], ACT.Gelu, bias=p1b).then_inc(gelu_done, 1)

            layernorm(1)
            swiglu(0)
            layernorm(2)

            for i in range(2 * NT):
                t, half = divmod(i, 2)
                act.wait_ge(v_done, i + 1)
                nc.scalar.activation(v_all[:, half * 8:half * 8 + 8, t, 0:DH],
                                     ps[:, i % 4, :].rearrange("p (h d) -> p h d", d=DH), ACT.Copy
                                     ).then_inc(v_hi_done, 1)

            def tick(g, p, last, first=False):
                c = g * PAIR + p
                src = s_ps[:, p % 2, :, :].rearrange("p k n -> p (k n)")
                act.wait_ge(scores_done, c + 1)
                if not (first and p < RING):
                    q = p - RING
                    owner = low_on_dve(q % PAIR, last)
                    act.wait_ge(lo_dve if owner else lo_pool, g * LOW_PAIR[owner] + low_count(q, last, owner))
                nc.scalar.activation(p32[:, p % RING, :], src, ACT.Exp, scale=DH ** -0.5).then_inc(exp_done, 1)
                if not (first and p < RING):
                    act.wait_ge(pv_done, c - RING + 1)
                nc.scalar.activation(p_hi[:, p % RING, :], src, ACT.Exp, scale=DH ** -0.5).then_inc(hi_done, 1)

            act.wait_ge(normed, 3 * NB)
            for p in range(ROT):
                tick(0, p, False, first=True)
            with act.Fori(0, NP - 1) as g:
                for p in range(ROT, ROT + PAIR):
                    tick(g, p, False)
            for p in range(ROT, PAIR):
                tick(NP - 1, p, True)

            layernorm(3)
            swiglu(1)

        @block.vector
        def _(dve):
            steps = {"n": 0, "g": None, "per": 0}

            def step_wait(k):
                steps["n"] += k
                dve.wait_ge(dve_step, steps["n"] if steps["g"] is None else steps["g"] * steps["per"] + steps["n"])

            def link(ins):
                ins.then_inc(dve_step, 1)
                step_wait(1)

            def cols(b):
                return slice(b * BLK, (b + 1) * BLK)

            def layernorm(k):
                for b in range(NB):
                    dve.wait_ge(rooted, NB * k + b + 1)
                    link(nc.vector.reciprocal(ln_std[:, b, :], ln_std[:, b, :]))
                    nc.vector.tensor_tensor(xnT[:, cols(b)], ps[:, b, :], ln_std[:, b, :], ALU.mult
                                            ).then_inc(normed, 1)

            def swiglu(f):
                n = NB * FH

                def down(b):
                    dve.wait_ge(down_done, NB * f + b + 1)
                    nc.vector.tensor_tensor(xT[:, cols(b)], ps[:, b, :], xT[:, cols(b)], ALU.add
                                            ).then_inc(x_new, 1)

                for i in range(n):
                    b, j = divmod(i, FH)
                    dve.wait_ge(silu_done, n * f + i + 1)
                    if b >= 2 and j == 0:
                        dve.wait_ge(down_done, NB * f + b - 1)
                    nc.vector.tensor_tensor(ff_h[:, (b % 2) * FH + j, :], ps[:, 5 + 2 * (i % 2), :], ff_s[:, i % 2, :],
                                            ALU.mult).then_inc(h_done, 1)
                    if j == 2 and b:
                        down(b - 1)
                down(NB - 1)

            nc.vector.memset(eps[:], EPS)
            for i in range(2):
                link(nc.vector.memset(k2[i][0:DH, :].bitcast(F32), 0.0))
                nc.vector.memset(k2[i][0:1, :].bitcast(F32), 1.0)
            dve.wait_ge(vw_in, 16)
            link(nc.vector.tensor_tensor(wv_sq, wv, wv, ALU.mult))
            nc.vector.tensor_reduce(v_norm[:], wv_sq, AX, ALU.add).then_inc(v_summed, 1)
            dve.wait_ge(ff_in, 48)
            nc.vector.tensor_scalar(wgu[:], ints[:, 0:2 * FH, :], 1.0 / 127.0, None, ALU.mult)
            nc.vector.tensor_scalar(wd[:], ints[:, 2 * FH:3 * FH, :], 1.0 / 127.0, None, ALU.mult
                                    ).then_inc(ff_ready, 1)
            dve.wait_ge(v_rooted, 1)
            link(nc.vector.tensor_scalar(v_norm[:], v_norm[:], 1e-30, None, ALU.max))
            link(nc.vector.tensor_scalar(v_pow[:].bitcast(I32), v_norm[:].bitcast(I32), 0x7F800000, None,
                                         ALU.bitwise_and))
            nc.vector.tensor_scalar(v_unscale[:], v_pow[:], 1.0 / V_LIMIT, None, ALU.mult)
            link(nc.vector.reciprocal(v_scale[:], v_pow[:]))
            link(nc.vector.tensor_scalar(v_scale[:], v_scale[:], V_LIMIT, None, ALU.mult))
            nc.vector.tensor_tensor(wv, wv, v_scale[:].unsqueeze(2).broadcast_to([P, NP, C]), ALU.mult
                                    ).then_inc(wv_scaled, 1)

            dve.wait_ge(a_in, 16 * (14 + C // HD))
            w8 = wkv.rearrange("p s (h d) -> p (s h) d", d=HD)
            link(nc.vector.tensor_reduce(wkv_mean, w8, AX, ALU.add))
            link(nc.vector.scalar_tensor_tensor(w8, wkv_mean.unsqueeze(2).broadcast_to([P, 64, HD]), -1.0 / HD, w8,
                                                ALU.mult, ALU.add))
            for s in range(2):
                for dst, i in ((gamma, s), (beta, 2 + s)):
                    last = nc.vector.tensor_copy(dst[:, s * C:(s + 1) * C].rearrange("p (h d) -> p h d", d=HD),
                                                 gb8[:, i, :].unsqueeze(1).broadcast_to([P, C // HD, HD]))
            last.then_inc(gamma_ready, 1)
            nc.vector.tensor_tensor(kv_bias.rearrange("p (h e) -> p h e", e=HD),
                                    mask.rearrange("p (h e) -> p h e", e=HD),
                                    kv_bias8.unsqueeze(1).broadcast_to([P, C // HD, HD]), ALU.mult)
            link(nc.vector.tensor_scalar(temp, temp, 1.0 / T, None, ALU.mult))
            layernorm(0)

            def kv_move(u):
                dve.wait_ge(kv_done, u + 1)
                nc.vector.tensor_tensor(kv[:, 4 * u:4 * u + 4, :],
                                        ps[:, 2 * u:2 * u + 2, :].rearrange("p b (t n) -> p (b t) n", n=256),
                                        wkv[:, 1, :].unsqueeze(1).broadcast_to([P, 4, 256]), ALU.add
                                        ).then_inc(kv_moved, 1)

            def groups(u):
                return kv[:, 4 * u:4 * u + 4, :].rearrange("p t (h d) -> p (t h) d", d=HD)

            def kv_sum(u):
                dve.wait_ge(kv_squared, u + 1)
                nc.vector.tensor_reduce(kv_rstd[:, u, :], kv_sq[:, u % 2, :].rearrange("p (g d) -> p g d", d=HD),
                                        AX, ALU.add).then_inc(kv_summed, 1)

            def kv_norm(u):
                dve.wait_ge(kv_rooted, u + 1)
                link(nc.vector.reciprocal(kv_rstd[:, u, :], kv_rstd[:, u, :]))
                nc.vector.tensor_tensor(groups(u), groups(u),
                                        kv_rstd[:, u, :].unsqueeze(2).broadcast_to([P, 128, HD]), ALU.mult
                                        ).then_inc(kv_scaled, 1)

            def kv_beta(u):
                dve.wait_ge(kv_gamma, u + 1)
                nc.vector.tensor_tensor(kv[:, 4 * u:4 * u + 4, :], kv[:, 4 * u:4 * u + 4, :],
                                        beta.unsqueeze(1).broadcast_to([P, 4, 256]), ALU.add).then_inc(kv_ready, 1)

            kv_move(0)
            kv_move(1)
            kv_sum(0)
            kv_norm(0)
            kv_move(2)
            kv_move(3)
            for u in range(1, 4):
                kv_sum(u)
                kv_norm(u)
                kv_beta(u - 1)
            dve.wait_ge(wv_turned, 1)
            nc.vector.tensor_copy(wvT.rearrange("p (b n) -> p b n", b=2), ps[:, 5:7, :])
            nc.vector.tensor_scalar(y_bias[:], ps[:, 7, 0:1], out_b[:], None, ALU.add).then_inc(wv_ready, 1)
            kv_beta(3)
            dve.wait_ge(kvprod_done, 1)
            link(nc.vector.scalar_tensor_tensor(kv_bd, ps[:, 4, 0:P], temp, mask, ALU.mult, ALU.mult))
            nc.vector.tensor_tensor(kv_bd, kv_bd, kv_bias, ALU.add).then_inc(kv_bd_ready, 1)

            def att_move(b):
                dve.wait_ge(att_done, b + 1)
                nc.vector.tensor_tensor(attT[:, cols(b)], ps[:, b, :], xnT[:, cols(b)], ALU.add).then_inc(att_moved, 1)

            def a_out(b):
                link(nc.vector.tensor_tensor(xT[:, cols(b)], xT[:, cols(b)], xnT[:, cols(b)], ALU.add))
                dve.wait_ge(p2_done, b + 1)
                nc.vector.scalar_tensor_tensor(xT[:, cols(b)], ps[:, b, :], p2b, xT[:, cols(b)], ALU.add, ALU.add
                                               ).then_inc(x_new, 1)

            for b in range(NB):
                att_move(b)
            for b in range(NB):
                a_out(b)

            layernorm(1)
            swiglu(0)
            layernorm(2)
            link(nc.vector.tensor_scalar(xT[:], xT[:], y_bias[:], None, ALU.add))

            def take(job, bank, m, n):
                dve.wait_ge(aux_done, m + 1)
                src = aux_ps[:, bank, :]
                kind, i = job[0], job[1]
                if kind == "proj":
                    b = job[2]
                    link(nc.vector.tensor_scalar(k1[i][:, cols(b)], src, bkq[i][:], None, ALU.add))
                    if b % 2:
                        nc.vector.scalar_tensor_tensor(q2[i][:, cols(b)], src, bkq[i][:], f32(k1[i][:, cols(b)]),
                                                       ALU.add, ALU.subtract).then_inc(aux_used, 1)
                        dve.wait_ge(aux_used, m + 1)
                        dve.sem_inc(kq_split)
                    else:
                        nc.vector.scalar_tensor_tensor(q2[i][:, cols(b)], src, bkq[i][:], f32(k1[i][:, cols(b)]),
                                                       ALU.add, ALU.subtract).then_inc(aux_used, 1)
                elif kind == "max":
                    t, kb = max_operands(job[2])
                    ins = nc.vector.tensor_reduce(maxes[:, t, kb:kb + 1], src, AX, ALU.max).then_inc(aux_used, 1)
                    if job[2] == 4 * NT - 1:
                        dve.wait_ge(aux_used, m + 1)
                        link(nc.vector.tensor_reduce(row_max[:], maxes[:], AX, ALU.max))
                        nc.vector.tensor_scalar(neg_max[:], row_max[:], -1.0, P_SCALE * DH ** 0.5, ALU.mult, ALU.add
                                                ).then_inc(neg_max_ready, 1)
                elif kind == "shift":
                    if not (isinstance(n, int) and n < 0):
                        dve.wait_ge(shift_in, n * 16 + 16)
                    nc.vector.tensor_copy(shift[:], src[0:NT, 0:P]).then_inc(aux_used, 1)
                    dve.wait_ge(aux_used, m + 1)
                    dve.sem_inc(shift_ready)
                elif kind == "turn":
                    nc.vector.tensor_scalar(oT[:], src, unscale[:], None, ALU.mult).then_inc(aux_used, 1)
                else:
                    nc.vector.tensor_tensor(xT[:, cols(job[1])], src, xT[:, cols(job[1])], ALU.add
                                            ).then_inc(aux_used, 1)

            def v_low(i):
                t, half = divmod(i, 2)
                dve.wait_ge(v_hi_done, i + 1)
                nc.vector.tensor_tensor(v_all[:, half * 8:half * 8 + 8, t, DH + 1:VW],
                                        ps[:, i % 4, :].rearrange("p (h d) -> p h d", d=DH),
                                        v_all[:, half * 8:half * 8 + 8, t, 0:DH], ALU.subtract).then_inc(v_lo_done, 1)

            dve.wait_ge(w_in[0], 32)
            for b in range(NB):
                take(("proj", 0, b), b % 2, b, -1)
            AHEAD = 8
            for i in range(2 * NT):
                v_low(i)
                if i >= AHEAD:
                    for n in (2 * (i - AHEAD), 2 * (i - AHEAD) + 1):
                        take(("max", 0, n), n % 2, NB + n, -1)
            for n in range(2 * (2 * NT - AHEAD), 4 * NT):
                take(("max", 0, n), n % 2, NB + n, -1)
            take(("shift", 0), (NB + 4 * NT) % 2, NB + 4 * NT, -1)

            def low(g, p, last):
                c = g * PAIR + p
                dve.wait_ge(hi_done, c + 1)
                if not (isinstance(c, int) and c < RING):
                    dve.wait_ge(pv_done, c - RING + 1)
                nc.vector.tensor_tensor(p_lo[:, p % RING, :], p32[:, p % RING, :], p_hi[:, p % RING, :], ALU.subtract
                                        ).then_inc(lo_dve, 1)

            def o_move(g, q):
                o4 = o_ps[:, :, 0:2 * VW].rearrange("p b (t v) -> p b t v", v=VW)
                qb, i = q // 8 % 4, q // HEAD % 2
                dst = o_sb[:, 4 * qb:4 * qb + 4, i * DH:(i + 1) * DH].rearrange("p (b t) d -> p b t d", b=2)
                dve.wait_ge(pv_done, g * PAIR + q + 1)
                nc.vector.tensor_copy(o_low[:], o4[:, :, :, DH + 1:VW]).then_inc(dve_step, 1)
                nc.vector.reciprocal(rden[:].unsqueeze(3), o4[:, :, :, DH:DH + 1]).then_inc(dve_step, 1)
                step_wait(1)
                nc.vector.tensor_tensor(o_low[:], o4[:, :, :, 0:DH], o_low[:], ALU.add).then_inc(o_read, 1)
                dve.wait_ge(o_read, g * 8 + q // 8 + 1)
                step_wait(1)
                nc.vector.tensor_tensor(dst, o_low[:], rden[:].unsqueeze(3).broadcast_to([P, 2, 2, DH]), ALU.mult
                                        ).then_inc(o_used, 1)

            def tick(g, p, last, first=False):
                jobs = first_jobs(p) if first else aux_jobs(p, last)
                done = aux_before(p, last, first)
                for k, job in enumerate(jobs):
                    m = done + k if first else g * AUX_PAIR + done + k
                    take(job, (done + k) % 2, m, g * 2 + p // HEAD)
                if p and low_on_dve((p - 1) % PAIR, last) and not (last and p - 1 >= PAIR):
                    low(g, p - 1, last)
                q = p - LAG
                if q >= 0 and q % 8 == 7 and not (last and q >= PAIR):
                    o_move(g, q)

            for p in range(ROT):
                tick(0, p, False, first=True)
            steps["per"] = 8 + 2 * 8 + 2
            with dve.Fori(0, NP - 1) as g:
                steps["g"], before = g, steps["n"]
                for p in range(ROT, ROT + PAIR):
                    tick(g, p, False)
                assert steps["n"] - before == steps["per"], steps["n"] - before
            steps["g"], steps["n"] = None, before + (NP - 1) * steps["per"]
            for p in range(ROT, ROT + PAIR):
                tick(NP - 1, p, True)

            layernorm(3)
            swiglu(1)

        @block.gpsimd
        def _(pool):
            for u in range(4):
                pool.wait_ge(kv_scaled, u + 1)
                nc.gpsimd.tensor_tensor(kv[:, 4 * u:4 * u + 4, :], kv[:, 4 * u:4 * u + 4, :],
                                        gamma.unsqueeze(1).broadcast_to([P, 4, 256]), ALU.mult).then_inc(kv_gamma, 1)
            pool.wait_ge(x_new, 2 * NB)
            nc.gpsimd.memset(v_all[:, :, :, DH:DH + 1], 1.0).then_inc(ones_done, 1)

            def tick(g, p, last, first=False):
                if low_on_dve(p % PAIR, last):
                    return
                c = g * PAIR + p
                pool.wait_ge(hi_done, c + 1)
                if not (first and p < RING):
                    pool.wait_ge(pv_done, c - RING + 1)
                nc.gpsimd.tensor_tensor(p_lo[:, p % RING, :], p32[:, p % RING, :], p_hi[:, p % RING, :], ALU.subtract
                                        ).then_inc(lo_pool, 1)

            for p in range(ROT):
                tick(0, p, False, first=True)
            with pool.Fori(0, NP - 1) as g:
                for p in range(ROT, ROT + PAIR):
                    tick(g, p, False)
            for p in range(ROT, PAIR):
                tick(NP - 1, p, True)


def kernel(**inputs):
    import numpy as np
    import concourse.bacc as bacc
    from concourse.bass_utils import run_bass_kernel_spmd as run

    x = {k.replace("L0_", ""): np.asarray(v) for k, v in inputs.items()}
    C, T, H2, H = 128, x["attn_a_x"].shape[1], 16, 16
    W, bW = x["attn_b_W_w"], x["attn_b_W_b"]
    D = H2 * DH
    by_head = lambda w: w.reshape(H2, DH, *w.shape[1:])
    arrays = {
        "xT": x["attn_a_x"][0].T,
        "wqkvT": x["attn_a_qkv_w"].T, "qkvb": x["attn_a_qkv_b"],
        "kn_g": x["attn_a_kn_g"], "vn_g": x["attn_a_vn_g"], "kn_b": x["attn_a_kn_b"], "vn_b": x["attn_a_vn_b"],
        "temperature": x["attn_a_temperature"], "attn_bias": x["attn_a_attn_bias"],
        "p1T": x["attn_a_p1_w"].T, "p1b": x["attn_a_p1_b"], "p2T": x["attn_a_p2_w"].T, "p2b": x["attn_a_p2_b"],
        "wkq": np.concatenate([by_head(W[D:2 * D]), by_head(W[0:D])], axis=1).transpose(0, 2, 1),
        "bkq": np.concatenate([by_head(bW[D:2 * D]), by_head(bW[0:D])], axis=1),
        "wv": W[2 * D:], "bv": bW[2 * D:].reshape(D // C, C).T, "woT": x["attn_b_out_w"].T, "outb": x["attn_b_out_b"],
        "wg": x["ffn_w_gate"].T, "wu": x["ffn_w_up"].T, "wd": x["ffn_w_down"].T,
        "ident": np.eye(C, dtype=np.float32),
        "centre": np.eye(C, dtype=np.float32) - np.float32(1.0 / C),
        "mean": np.full((C, C), 1.0 / C, np.float32),
        "mask": np.kron(np.eye(H, dtype=np.float32), np.ones((C // H, C // H), np.float32)),
    }
    nc = bacc.Bacc("TRN2", target_bir_lowering=False, num_devices=1)
    maps, args = {}, {}
    for name, v in arrays.items():
        v = np.ascontiguousarray(v)
        maps[f"in_{name}"] = v
        args[name] = nc.dram_tensor(f"in_{name}", v.shape, mybir.dt.from_np(v.dtype), kind="ExternalInput").ap()
    args["out"] = nc.dram_tensor("out_xT", (C, T), F32, kind="ExternalOutput").ap()
    block_program(nc, args)
    r = run(nc, [maps], core_ids=[0])
    return np.ascontiguousarray(np.asarray(r.results[0]["out_xT"]).T).reshape(1, T, C)
```

```python
import math
from contextlib import ExitStack

import concourse.bass as bass
from concourse import mybir

F32 = mybir.dt.float32
F32R = mybir.dt.float32r
F16 = mybir.dt.float16
I32 = mybir.dt.int32
ALU = mybir.AluOpType
ACT = mybir.ActivationFunctionType
AX = mybir.AxisListType.X

P = 128
EPS = 1e-5
BLK = 512
DH = 64
HD = 8
VW = 2 * DH + 1
LAG = 3
RING = 4
P_SCALE = math.log(32.0)
V_LIMIT = 2.0 ** 13

PAIR = 64
HEAD = 32
ROT = 6
MAX_FROM = 5
SIDE = 3
SHIFT_AT = 29
LOW_DVE = (2, 29)


def aux_jobs(p, last):
    v, parity = p % HEAD, (p // HEAD + 1) % 2
    jobs = []
    for b in range(4):
        if p % PAIR == (HEAD + 8 * b + 12) % PAIR:
            jobs.append(("turn", b))
        if p % PAIR == (HEAD + 8 * b + 13) % PAIR:
            jobs.append(("out", b))
    if last and p >= HEAD:
        return jobs
    if v < 2:
        jobs += [("proj", parity, 2 * v), ("proj", parity, 2 * v + 1)]
    if MAX_FROM <= v < SHIFT_AT:
        n = sum(SIDE - len(aux_jobs(p - v + u + PAIR, True)) for u in range(MAX_FROM, v))
        jobs = [("max", parity, k) for k in range(n, min(64, n + SIDE - len(jobs)))] + jobs
    if v == SHIFT_AT:
        jobs.append(("shift", parity))
    return jobs


def max_operands(n):
    return (n // 2, n % 2) if n < 16 else (8 + (n - 16) // 2, n % 2) if n < 32 else ((n - 32) // 2, 2 + n % 2)


def low_on_dve(p, last):
    if last and HEAD <= p:
        return p % 3 == 1
    return p % HEAD in LOW_DVE


def block_program(nc, a):
    T = a["xT"].shape[1]
    C = P
    NT, NB = T // P, T // BLK
    H2 = a["wkq"].shape[0]
    NP = H2 // 2
    FH = a["wd"].shape[0] // P
    assert T == 2048 and a["xT"].shape[0] == C and H2 * DH == 1024 and FH == 3

    with ExitStack() as ctx:
        def sb(name, shape, dt=F32):
            return ctx.enter_context(nc.sbuf_tensor(name, shape, dt))

        def sem(name):
            return ctx.enter_context(nc.semaphore(name))

        ps = ctx.enter_context(nc.psum_tensor("ps", [P, 8, BLK], F32))
        s_ps = ps[:, 0:4, :].rearrange("p (r k) n -> p r k n", r=2)
        o_ps = ps[:, 4:6, :]
        def aux_bank(m, first=False):
            return 4 + m % 4 if first else 6 + m % 2


        xT = sb("xT_sb", [P, T])
        xnT = sb("xnT", [P, T])
        consts = sb("consts", [P, 4, P])
        ident, centre, mean, first_row = (consts[:, i, :] for i in range(4))
        columns = sb("columns", [P, 5 + HD + 8])
        bq, p1b, p2b, out_b, temp = (columns[:, i:i + 1] for i in range(5))
        kv_bias8, v_bias = columns[:, 5:5 + HD], columns[:, 5 + HD:]
        eps = sb("eps", [P, 1])
        k1 = [sb(f"k1_{i}", [P, T], F32R) for i in range(2)]
        k2 = [sb(f"k2_{i}", [P, T], F32R) for i in range(2)]
        q1 = [sb(f"q1_{i}", [P, T], F32R) for i in range(2)]
        q2 = [sb(f"q2_{i}", [P, T], F32R) for i in range(2)]
        v_flat = sb("v_all", [P, H2 * NT * VW], F16)
        v_all = v_flat[:].rearrange("p (h t v) -> p h t v", h=H2, t=NT)
        v_head = [sb(f"v_head{i}", [P, NT, VW], F16) for i in range(2)]
        wkq = [sb(f"wkq{i}", [P, P]) for i in range(2)]
        bkq = [sb(f"bkq{i}", [P, 1]) for i in range(2)]
        wo = sb("wo_pair", [P, C])
        unscale = sb("unscale", [P, 1])
        p32 = sb("p32", [P, RING, 2 * BLK])
        p_hi = sb("p_hi", [P, RING, 2 * BLK], F16)
        p_lo = sb("p_lo", [P, RING, 2 * BLK], F16)
        maxes = sb("maxes", [P, NT, NB])
        row_max = sb("row_max", [P, NT])
        neg_max = sb("neg_max", [P, NT])
        shift = sb("shift", [NT, P], F32R)
        rden = sb("rden", [P, 2, 2])
        o_raw = sb("o_raw", [P, 2, 2, VW])
        o_sb = sb("o_sb", [P, NT, 2 * DH])
        oT = sb("oT", [P, BLK])
        v_unscale = sb("v_unscale", [P, NP])
        y_bias = sb("y_bias", [P, 1])
        idle = sb("idle", [P, 1])
        v_norm = sb("v_norm", [P, NP])
        v_pow = sb("v_pow", [P, NP])
        v_scale = sb("v_scale", [P, NP])
        wgu = sb("wgu", [P, 2 * FH, P])
        wd = sb("wd", [P, FH, P])

        room = v_flat[:].bitcast(F32)
        at = [0]

        def carve(n):
            at[0] += n
            assert at[0] <= room.shape[1]
            return room[:, at[0] - n:at[0]]

        kv = carve(NT * 256).rearrange("p (t n) -> p t n", n=256)
        kv_sq = carve(2048).rearrange("p (r n) -> p r n", r=2)
        qT, attT, hT = carve(T), carve(T), carve(T)
        w_a = carve(5 * P)
        rows = carve(4 * HD + 256)
        gb8 = rows[:, 0:4 * HD].rearrange("p (s n) -> p s n", n=HD)
        wkv, wkv_b = w_a[:, 0:256], rows[:, 4 * HD:]
        wq, p1w, p2w = (w_a[:, 256 + i * P:256 + (i + 1) * P] for i in range(3))
        wkv_mean = carve(64)
        mask = carve(P)
        gamma, beta = carve(256), carve(256)
        kv_rstd = carve(4 * 128).rearrange("p (u n) -> p u n", u=4)
        kv_bd, kv_bias = carve(P), carve(P)
        ff_room = room[:, 0:6 * BLK + 2 * BLK]
        ff_h = ff_room[:, 0:6 * BLK].rearrange("p (r n) -> p r n", r=6)
        ff_s = ff_room[:, 6 * BLK:8 * BLK].rearrange("p (r n) -> p r n", r=2)
        wv = p_hi[:].rearrange("p r n -> p (r n)").bitcast(F32)[:, 0:1024].rearrange("p (j c) -> p j c", c=C)
        wv_sq = p_hi[:].rearrange("p r n -> p (r n)").bitcast(F32)[:, 1024:2048].rearrange("p (j c) -> p j c", c=C)
        ints = p_lo[:].rearrange("p r n -> p (r n)").bitcast(I32)[:, 0:3 * FH * P].rearrange("p (j c) -> p j c", c=P)
        wvT = o_sb[:].rearrange("p t n -> p (t n)")[:, 0:1024]
        woT = o_sb[:].rearrange("p t n -> p (t n)")[:, 1024:2048].rearrange("p (j c) -> p j c", c=C)
        ln_sq = p32[:, :, 0:BLK]
        ln_std = p32[:, 0, BLK:2 * BLK]
        v32 = p32[:].rearrange("p r n -> p (r n)").rearrange("p (s n) -> p s n", n=BLK)

        def f32(ap):
            return ap.bitcast(F32)

        x_in = [sem(f"x_in{b}") for b in range(NB)]
        const_in, a_in, ff_in, vw_in, bias_in = (
            sem(n) for n in ("const_in", "a_in", "ff_in", "vw_in", "bias_in"))
        dve_step = sem("dve_step")
        centred, squared, averaged, rooted, inverted, spread_std, normed = (
            sem(n) for n in ("centred", "squared", "averaged", "rooted", "inverted", "spread_std", "normed"))
        kv_done, kv_moved, kv_squared, kv_summed, kv_rooted, kv_scaled, kv_gamma, kv_ready = (
            sem(n) for n in ("kv_done", "kv_moved", "kv_squared", "kv_summed", "kv_rooted", "kv_scaled",
                             "kv_gamma", "kv_ready"))
        zeros_done = sem("zeros_done")
        gamma_ready, q_done, q_moved, kvprod_done, kv_bd_ready = (
            sem(n) for n in ("gamma_ready", "q_done", "q_moved", "kvprod_done", "kv_bd_ready"))
        att_done, att_moved, p1_done, gelu_done, p2_done, x_new = (
            sem(n) for n in ("att_done", "att_moved", "p1_done", "gelu_done", "p2_done", "x_new"))
        ff_ready, gu_done, silu_done, h_done, down_done = (
            sem(n) for n in ("ff_ready", "gu_done", "silu_done", "h_done", "down_done"))
        v_summed, v_rooted, wv_scaled, wv_turned, wv_ready, v_done, v_moved, v_lo_done, ones_done = (
            sem(n) for n in ("v_summed", "v_rooted", "wv_scaled", "wv_turned", "wv_ready", "v_done",
                             "v_moved", "v_lo_done", "ones_done"))
        w_in = [sem(f"w_in{i}") for i in range(2)]
        v_in = [sem(f"v_in{i}") for i in range(2)]
        wo_in = sem("wo_in")
        kq_split = sem("kq_split")
        spread_hi = sem("spread_hi")
        spread_lo = [sem(f"spread_lo{i}") for i in range(2)]
        shift_ready, shift_in = sem("shift_ready"), sem("shift_in")
        neg_max_ready = sem("neg_max_ready")
        aux_done, aux_used = sem("aux_done"), sem("aux_used")
        scores_done, exp_done, hi_done = sem("scores_done"), sem("exp_done"), sem("hi_done")
        lo_pool, lo_dve = sem("lo_pool"), sem("lo_dve")
        pv_done, o_read, o_used = sem("pv_done"), sem("o_read"), sem("o_used")
        stored = sem("stored")

        AUX_PAIR = sum(len(aux_jobs(p, False)) for p in range(ROT, ROT + PAIR))
        def first_jobs(p):
            return [j for j in aux_jobs(p, False) if j[0] in ("proj", "max", "shift")]

        PROLOGUE = [j for p in range(ROT) for j in first_jobs(p)]
        AUX_FIRST = NB + 4 * NT + 1
        assert AUX_PAIR % 2 == 0

        def aux_before(p, last, first=False):
            if first:
                return AUX_FIRST + sum(len(first_jobs(q)) for q in range(p))
            return AUX_FIRST + len(PROLOGUE) + sum(len(aux_jobs(q, last)) for q in range(ROT, p))

        def low_count(p, last, dve):
            return sum(low_on_dve(q % PAIR, last) == dve for q in range(p + 1))

        LOW_PAIR = {dve: low_count(PAIR - 1, False, dve) for dve in (True, False)}

        block = ctx.enter_context(nc.Block())

        @block.sync
        def _(sp):
            for b in range(NB):
                sp.dma_start(xT[:, b * BLK:(b + 1) * BLK], a["xT"][:, b * BLK:(b + 1) * BLK]).then_inc(x_in[b], 16)
            sp.dma_start(w_a, a["w_a"]).then_inc(a_in, 16)
            sp.dma_start(rows, a["rows"].rearrange("(o n) -> o n", o=1).broadcast_to([P, 4 * HD + 256])
                         ).then_inc(a_in, 16)
            sp.dma_start(mask, a["mask"]).then_inc(a_in, 16)

            def load_w(i, n):
                sp.dma_start(wkq[i][:], a["wkq"][bass.ds(n, 1), :, :].rearrange("o c m -> (o c) m")
                             ).then_inc(w_in[i], 16)
                sp.dma_start(bkq[i][:], a["bkq"][bass.ds(n, 1), :].rearrange("o (m u) -> (o m) u", u=1)
                             ).then_inc(w_in[i], 16)

            def load_v(i, n):
                sp.dma_start(v_head[i][:].rearrange("p t v -> p (t v)"),
                             v_all[:, bass.ds(n, 1), :, :].rearrange("p o t v -> p (o t v)")).then_inc(v_in[i], 16)

            def load_wo(g):
                sp.dma_start(wo[:], a["woT"][bass.ds(g * P, P), :]).then_inc(wo_in, 16)
                sp.dma_start(unscale[:], v_unscale[:, bass.ds(g, 1)]).then_inc(wo_in, 16)

            def spread(i, n, half):
                cols = slice(half * T // 2, (half + 1) * T // 2)
                sp.wait_ge(kq_split, n * 2 + half + 1)
                sp.dma_start(f32(q1[i][0:DH, cols]), f32(k1[i][DH:P, cols])).then_inc(spread_hi, 16)
                sp.dma_start(f32(q1[i][DH:P, cols]), f32(k1[i][DH:P, cols])).then_inc(spread_hi, 16)
                sp.dma_start(f32(k2[i][DH:P, cols]), f32(k1[i][0:DH, cols])).then_inc(spread_hi, 16)
                sp.wait_ge(spread_hi, n * 96 + half * 48 + 48)
                sp.dma_start(f32(k1[i][DH:P, cols]), f32(q2[i][0:DH, cols])).then_inc(spread_lo[half], 16)

            def place_shift(i, n):
                sp.wait_ge(shift_ready, n + 1)
                for half in range(2):
                    sp.wait_ge(spread_lo[half], n * 16 + 16)
                sp.dma_start(f32(q2[i][0:1, :]).rearrange("o (t n) -> o t n", t=NT), f32(shift[:])).then_inc(shift_in, 16)

            load_w(0, 0)
            load_w(1, 1)
            for half in range(2):
                spread(0, 0, half)
            place_shift(0, 0)
            sp.wait_ge(v_lo_done, 2 * NT)
            sp.wait_ge(ones_done, 3)
            load_v(0, 0)
            load_v(1, 1)
            load_wo(0)
            for half in range(2):
                spread(1, 1, half)

            def pair_moves(g, last):
                if not last:
                    load_w(0, g * 2 + 2)
                place_shift(1, g * 2 + 1)
                if last:
                    return
                for half in range(2):
                    spread(0, g * 2 + 2, half)
                load_w(1, g * 2 + 3)
                sp.wait_ge(pv_done, g * PAIR + HEAD)
                load_v(0, g * 2 + 2)
                place_shift(0, g * 2 + 2)
                for half in range(2):
                    spread(1, g * 2 + 3, half)
                sp.wait_ge(pv_done, g * PAIR + PAIR)
                load_v(1, g * 2 + 3)
                sp.wait_ge(aux_used, g * AUX_PAIR + aux_before(ROT + PAIR, False))
                load_wo(g + 1)

            with sp.Fori(0, NP - 1) as g:
                pair_moves(g, False)
            pair_moves(NP - 1, True)
            for b in range(NB):
                sp.wait_ge(x_new, 2 * NB + b + 1)
                sp.dma_start(a["out"][:, b * BLK:(b + 1) * BLK], xT[:, b * BLK:(b + 1) * BLK]).then_inc(stored, 16)
            sp.wait_ge(stored, 16 * NB)

        @block.tensor
        def _(pe):
            def cols(b):
                return slice(b * BLK, (b + 1) * BLK)

            def layernorm(k, x_ready):
                def average(b):
                    pe.wait_ge(squared, NB * k + b + 1)
                    pe.matmul(ps[32 * b:32 * b + 32, 7, :], mean[:, 0:32], ln_sq[:, b, :], start=True, stop=True
                              ).then_inc(averaged, 1)

                for b in range(NB):
                    pe.wait_ge(*x_ready(b))
                    pe.matmul(ps[:, b, :], centre, xT[:, cols(b)], start=True, stop=True).then_inc(centred, 1)
                    if b:
                        average(b - 1)
                average(NB - 1)
                for _ in range(5):
                    pe.matmul(ps[:, 4, :], centre, xT[:, cols(0)], start=True, stop=True)
                pe.wait_ge(inverted, k + 1)
                for b in range(NB):
                    pe.matmul(ps[:, 4 + b, :], first_row[32 * b:32 * b + 32, :], ln_std[32 * b:32 * b + 32, :],
                              start=True, stop=True).then_inc(spread_std, 1)

            def swiglu(f, k):
                n = NB * FH

                def down(b):
                    pe.wait_ge(h_done, n * f + FH * (b + 1))
                    for j in range(FH):
                        last = pe.matmul(ps[:, b, :], wd[:, j, :], ff_h[:, (b % 2) * FH + j, :],
                                         start=(j == 0), stop=(j == FH - 1))
                    last.then_inc(down_done, 1)

                for i in range(n):
                    b, j = divmod(i, FH)
                    pe.wait_ge(normed, NB * k + (2 if i == 0 else NB))
                    if i >= 2:
                        pe.wait_ge(h_done, n * f + i - 1)
                    bank = 4 + 2 * (i % 2)
                    pe.matmul(ps[:, bank, :], wgu[:, j, :], xnT[:, cols(b)], start=True, stop=True)
                    pe.matmul(ps[:, bank + 1, :], wgu[:, FH + j, :], xnT[:, cols(b)], start=True, stop=True
                              ).then_inc(gu_done, 1)
                    if j == 1 and b:
                        down(b - 1)
                down(NB - 1)

            pe.wait_ge(const_in, 16)
            layernorm(0, lambda b: (x_in[b], 16))
            pe.wait_ge(gamma_ready, 1)
            for u in range(4):
                pe.wait_ge(normed, 2 if u == 0 else NB)
                for t in range(4 * u, 4 * u + 4):
                    last = pe.matmul(ps[:, t // 2, (t % 2) * 256:(t % 2) * 256 + 256], xnT[:, t * P:(t + 1) * P],
                                     wkv, start=True, stop=True, skip_group_check=True)
                last.then_inc(kv_done, 1)
            for b in range(NB):
                pe.wait_ge(kv_moved, b // 2 + 1)
                pe.matmul(ps[:, b, :], wq, xnT[:, cols(b)], start=True, stop=True).then_inc(q_done, 1)
            pe.wait_ge(kv_moved, 4)
            pe.wait_ge(wv_scaled, 1)
            for j in range(NP):
                pe.transpose(ps[:, 5 + j // 4, (j % 4) * P:(j % 4 + 1) * P], wv[:, j, :], ident)
            pe.wait_ge(bias_in, 32)
            for j in range(NP):
                last = pe.matmul(ps[:, 7, 0:1], woT[:, j, :], v_bias[:, j:j + 1], start=(j == 0), stop=(j == NP - 1))
            last.then_inc(wv_turned, 1)
            for t in range(NT):
                pe.wait_ge(kv_ready, t // 4 + 1)
                last = pe.matmul(ps[:, 4, 0:P], kv[:, t, 0:P], kv[:, t, P:2 * P], start=(t == 0), stop=(t == NT - 1))
            last.then_inc(kvprod_done, 1)
            pe.wait_ge(kv_bd_ready, 1)
            pe.wait_ge(wv_ready, 1)
            for s in range(NB + 2):
                if s < NB:
                    pe.wait_ge(q_moved, s + 1)
                    pe.matmul(ps[:, s, :], kv_bd, qT[:, cols(s)], start=True, stop=True).then_inc(att_done, 1)
                if 1 <= s <= NB:
                    pe.wait_ge(att_moved, s)
                    pe.matmul(ps[:, 3 + s, :], p1w, attT[:, cols(s - 1)], start=True, stop=True).then_inc(p1_done, 1)
                if s >= 2:
                    pe.wait_ge(gelu_done, s - 1)
                    pe.matmul(ps[:, s - 2, :], p2w, hT[:, cols(s - 2)], start=True, stop=True).then_inc(p2_done, 1)

            layernorm(1, lambda b: (x_new, b + 1))
            pe.wait_ge(ff_ready, 1)
            swiglu(0, 1)
            layernorm(2, lambda b: (x_new, NB + b + 1))

            def aux(job, bank):
                out = ps[:, bank, :]
                kind, i = job[0], job[1]
                if kind == "proj":
                    return pe.matmul(out, wkq[i][:], xnT[:, cols(job[2])], start=True, stop=True)
                if kind == "max":
                    t, kb = max_operands(job[2])
                    return pe.matmul(out, q1[i][:, t * P:(t + 1) * P], k1[i][:, cols(kb)], start=True, stop=True)
                if kind == "shift":
                    return pe.transpose(out[0:NT, 0:P], neg_max[:], ident)
                if kind == "turn":
                    for t in range(4):
                        last = pe.transpose(out[:, t * P:(t + 1) * P], o_sb[:, 4 * i + t, :], ident)
                    return last
                return pe.matmul(out, wo[:], oT[:], start=True, stop=True)

            def scores(p, kt):
                i, (qb, kp) = p // HEAD % 2, divmod(p % HEAD, 8)
                k = slice((2 * kp + kt) * P, (2 * kp + kt + 1) * P)
                out = s_ps[:, p % 2, kt, :]
                pe.matmul(out, k1[i][:, k], q1[i][:, cols(qb)], start=True, stop=False)
                last = pe.matmul(out, k2[i][:, k], q2[i][:, cols(qb)], start=False, stop=True)
                if kt == 1:
                    last.then_inc(scores_done, 1)

            def times_v(p):
                i, v = p // HEAD % 2, p % HEAD
                for kt in range(2):
                    k = 2 * (v % 8) + kt
                    for t in range(4):
                        at0 = (t % 2) * VW
                        w = slice(kt * BLK + t * P, kt * BLK + (t + 1) * P)
                        pe.matmul(o_ps[:, t // 2, at0:at0 + VW], p_hi[:, p % RING, w], v_head[i][:, k, :],
                                  start=(k == 0 and t % 2 == 0), stop=False, skip_group_check=True)
                        last = pe.matmul(o_ps[:, t // 2, at0:at0 + DH + 1], p_lo[:, p % RING, w],
                                         v_head[i][:, k, 0:DH + 1], start=False, stop=(k == NT - 1),
                                         skip_group_check=True)
                last.then_inc(pv_done, 1)

            pe.wait_ge(normed, 3 * NB)
            pe.wait_ge(w_in[0], 32)
            for b in range(NB):
                aux(("proj", 0, b), aux_bank(b, True)).then_inc(aux_done, 1)

            def first_max(n):
                if n == 0:
                    pe.wait_ge(spread_lo[0], 16)
                if n == 16:
                    pe.wait_ge(spread_lo[1], 16)
                pe.wait_ge(aux_used, NB + n - 3)
                aux(("max", 0, n), aux_bank(NB + n, True)).then_inc(aux_done, 1)

            AHEAD, WITH = 6, 3
            for i in range(2 * NT):
                t, half = divmod(i, 2)
                if i >= 4:
                    pe.wait_ge(v_moved, i - 3)
                pe.matmul(ps[:, i % 4, :], xnT[:, t * P:(t + 1) * P], wvT[:, half * BLK:(half + 1) * BLK],
                          start=True, stop=True).then_inc(v_done, 1)
                n = WITH * (i - AHEAD)
                for k in range(max(n, 0), min(n + WITH, 4 * NT)):
                    first_max(k)
                if n - WITH < 4 * NT <= n:
                    pe.wait_ge(neg_max_ready, 1)
                    aux(("shift", 0), aux_bank(NB + 4 * NT, True)).then_inc(aux_done, 1)

            def tick(g, p, last, first=False):
                c = g * PAIR + p
                n = g * 2 + p // HEAD
                jobs = first_jobs(p) if first else aux_jobs(p, last)
                done = aux_before(p, last, first)

                def side(k):
                    if k < 0:
                        return
                    job, m = jobs[k], done + k if first else g * AUX_PAIR + done + k
                    if job[0] == "proj" and job[2] == 0:
                        pe.wait_ge(w_in[job[1]], (g + (p // HEAD + 1) // 2) * 32 + 32)
                    for half in range(2):
                        if job[0] == "max" and job[2] == 16 * half:
                            pe.wait_ge(spread_lo[half], (n + 1) * 16 + 16)
                    if job[0] == "shift":
                        pe.wait_ge(neg_max_ready, n + 2)
                    if job[0] == "turn":
                        pe.wait_ge(o_used, g * 8 + 6 + job[1])
                    if job[0] == "out" and job[1] == 0:
                        pe.wait_ge(wo_in, g * 32 + 32)
                    after_turn = job[0] == "out" and k == 0 and len(jobs) < 3
                    pe.wait_ge(aux_used, m if after_turn else m - 1)
                    aux(job, aux_bank(done + k)).then_inc(aux_done, 1)

                first_side = len(jobs) - 3
                side(first_side)
                if not (last and p >= PAIR):
                    if p % HEAD == 0:
                        pe.wait_ge(shift_in, n * 16 + 16)
                    if first and p < 2:
                        pe.wait_ge(v_moved, 2 * NT)
                    else:
                        pe.wait_ge(hi_done, c - 1)
                    scores(p, 0)
                    side(first_side + 1)
                    scores(p, 1)
                else:
                    side(first_side + 1)
                side(first_side + 2)
                q = p - LAG
                with_v = not (first and q < 0) and not (last and q >= PAIR)
                if with_v:
                    if q % HEAD == 0:
                        pe.wait_ge(v_in[q // HEAD % 2], (g + q // PAIR) * 16 + 16)
                    if q % 8 == 0 and not (first and q == 0):
                        pe.wait_ge(o_read, g * 8 + q // 8)
                    owner = low_on_dve(q % PAIR, last)
                    pe.wait_ge(lo_dve if owner else lo_pool, g * LOW_PAIR[owner] + low_count(q, last, owner))
                    times_v(q)
                assert len(jobs) <= 3

            for p in range(ROT):
                tick(0, p, False, first=True)
            with pe.Fori(0, NP - 1) as g:
                for p in range(ROT, ROT + PAIR):
                    tick(g, p, False)
            for p in range(ROT, ROT + PAIR):
                tick(NP - 1, p, True)

            layernorm(3, lambda b: (aux_used, (NP - 1) * AUX_PAIR + aux_before(ROT + PAIR, True)))
            swiglu(1, 3)

        @block.scalar
        def _(act):
            act.dma_start(consts[:], a["consts"]).then_inc(const_in, 16)
            act.dma_start(wv, a["wv"].rearrange("(j p) c -> p j c", p=P)).then_inc(vw_in, 16)
            act.dma_start(columns[:], a["columns"]).then_inc(bias_in, 16)
            act.dma_start(ints[:, 0:2 * FH, :], a["wgu"]).then_inc(ff_in, 16)
            act.dma_start(ints[:, 2 * FH:3 * FH, :], a["wd"].rearrange("(j p) d -> p j d", p=P)).then_inc(ff_in, 16)
            act.dma_start(woT, a["woT"].rearrange("(j p) d -> p j d", p=P)).then_inc(bias_in, 16)

            def cols(b):
                return slice(b * BLK, (b + 1) * BLK)

            def load_table(f):
                nc.scalar.activation(idle[:], eps[:], f)

            def layernorm(k):
                if k:
                    load_table(ACT.Sqrt)
                for b in range(NB):
                    act.wait_ge(centred, NB * k + b + 1)
                    nc.scalar.activation(ln_sq[:, b, :], ps[:, b, :], ACT.Square).then_inc(squared, 1)
                act.wait_ge(averaged, NB * k + NB)
                if k == 0:
                    act.wait_ge(ff_ready, 1)
                nc.scalar.activation(ln_std, ps[:, 7, :], ACT.Sqrt, bias=eps[:]).then_inc(rooted, 1)

            def swiglu(f):
                n = NB * FH
                for i in range(n):
                    act.wait_ge(gu_done, n * f + i + 1)
                    if i >= 2:
                        act.wait_ge(h_done, n * f + i - 1)
                    nc.scalar.activation(ff_s[:, i % 2, :], ps[:, 4 + 2 * (i % 2), :], ACT.Silu).then_inc(silu_done, 1)

            act.wait_ge(v_summed, 1)
            nc.scalar.activation(v_norm[:], v_norm[:], ACT.Sqrt, scale=float(C)).then_inc(v_rooted, 1)

            layernorm(0)
            for u in range(4):
                act.wait_ge(kv_moved, u + 1)
                if u >= 2:
                    act.wait_ge(kv_summed, u - 1)
                nc.scalar.activation(kv_sq[:, u % 2, :], kv[:, 4 * u:4 * u + 4, :].rearrange("p t n -> p (t n)"),
                                     ACT.Square).then_inc(kv_squared, 1)
                act.wait_ge(q_done, u + 1)
                nc.scalar.activation(qT[:, cols(u)], ps[:, u, :], ACT.Identity, bias=bq).then_inc(q_moved, 1)
                act.wait_ge(kv_summed, u + 1)
                nc.scalar.activation(kv_rstd[:, u, :], kv_rstd[:, u, :], ACT.Sqrt, bias=eps[:], scale=1.0 / HD
                                     ).then_inc(kv_rooted, 1)
            for b in range(NB):
                act.wait_ge(p1_done, b + 1)
                nc.scalar.activation(hT[:, cols(b)], ps[:, 4 + b, :], ACT.Gelu, bias=p1b).then_inc(gelu_done, 1)

            layernorm(1)
            swiglu(0)
            layernorm(2)

            act.wait_ge(normed, 3 * NB)
            for i in range(2 * NT):
                t, half = divmod(i, 2)
                act.wait_ge(v_done, i + 1)
                nc.scalar.activation(v_all[:, half * 8:half * 8 + 8, t, 0:DH],
                                     ps[:, i % 4, :].rearrange("p (h d) -> p h d", d=DH), ACT.Copy)
                if i >= 8:
                    act.wait_ge(v_lo_done, i - 7)
                nc.scalar.activation(v32[:, i % 8, :], ps[:, i % 4, :], ACT.Copy).then_inc(v_moved, 1)

            def tick(g, p, last, first=False):
                c = g * PAIR + p
                q = p - LAG
                if not (last and p >= PAIR):
                    src = s_ps[:, p % 2, :, :].rearrange("p k n -> p (k n)")
                    act.wait_ge(scores_done, c + 1)
                    if not (first and p < RING):
                        r = p - RING
                        owner = low_on_dve(r % PAIR, last)
                        act.wait_ge(lo_dve if owner else lo_pool, g * LOW_PAIR[owner] + low_count(r, last, owner))
                    nc.scalar.activation(p32[:, p % RING, :], src, ACT.Exp, scale=DH ** -0.5).then_inc(exp_done, 1)
                if q >= 0 and q % 8 == 7 and not (last and q >= PAIR):
                    act.wait_ge(pv_done, g * PAIR + q + 1)
                    act.wait_ge(o_used, g * 8 + q // 8 + 1)
                    nc.scalar.activation(o_raw[:], o_ps[:, :, 0:2 * VW].rearrange("p b (t v) -> p b t v", v=VW),
                                         ACT.Copy).then_inc(o_read, 1)
                if not (last and p >= PAIR):
                    if not (first and p < RING):
                        act.wait_ge(pv_done, c - RING + 1)
                    nc.scalar.activation(p_hi[:, p % RING, :], src, ACT.Exp, scale=DH ** -0.5).then_inc(hi_done, 1)

            act.wait_ge(v_lo_done, 2 * NT)
            for p in range(ROT):
                tick(0, p, False, first=True)
            with act.Fori(0, NP - 1) as g:
                for p in range(ROT, ROT + PAIR):
                    tick(g, p, False)
            for p in range(ROT, ROT + PAIR):
                tick(NP - 1, p, True)

            layernorm(3)
            swiglu(1)

        @block.vector
        def _(dve):
            steps = {"n": 0, "g": None, "per": 0}

            def step_wait(k):
                steps["n"] += k
                dve.wait_ge(dve_step, steps["n"] if steps["g"] is None else steps["g"] * steps["per"] + steps["n"])

            def link(ins):
                ins.then_inc(dve_step, 1)
                step_wait(1)

            def cols(b):
                return slice(b * BLK, (b + 1) * BLK)

            def layernorm(k):
                for b in range(NB):
                    dve.wait_ge(squared, NB * k + b + 1)
                    nc.vector.tensor_copy(xnT[:, cols(b)], ps[:, b, :]).then_inc(dve_step, 1)
                dve.wait_ge(rooted, k + 1)
                nc.vector.reciprocal(ln_std, ln_std).then_inc(inverted, 1)
                step_wait(NB)
                for b in range(NB):
                    dve.wait_ge(spread_std, NB * k + b + 1)
                    nc.vector.tensor_tensor(xnT[:, cols(b)], ps[:, 4 + b, :], xnT[:, cols(b)], ALU.mult
                                            ).then_inc(normed, 1)

            def swiglu(f):
                n = NB * FH

                def down(b):
                    dve.wait_ge(down_done, NB * f + b + 1)
                    nc.vector.tensor_tensor(xT[:, cols(b)], ps[:, b, :], xT[:, cols(b)], ALU.add
                                            ).then_inc(x_new, 1)

                for i in range(n):
                    b, j = divmod(i, FH)
                    dve.wait_ge(silu_done, n * f + i + 1)
                    if b >= 2 and j == 0:
                        dve.wait_ge(down_done, NB * f + b - 1)
                    nc.vector.tensor_tensor(ff_h[:, (b % 2) * FH + j, :], ps[:, 5 + 2 * (i % 2), :], ff_s[:, i % 2, :],
                                            ALU.mult).then_inc(h_done, 1)
                    if j == 2 and b:
                        down(b - 1)
                down(NB - 1)

            nc.vector.memset(eps[:], EPS)
            dve.wait_ge(vw_in, 16)
            link(nc.vector.tensor_tensor(wv_sq, wv, wv, ALU.mult))
            nc.vector.tensor_reduce(v_norm[:], wv_sq, AX, ALU.add).then_inc(v_summed, 1)
            dve.wait_ge(ff_in, 32)
            nc.vector.tensor_scalar(wgu[:], ints[:, 0:2 * FH, :], 1.0 / 127.0, None, ALU.mult)
            nc.vector.tensor_scalar(wd[:], ints[:, 2 * FH:3 * FH, :], 1.0 / 127.0, None, ALU.mult
                                    ).then_inc(ff_ready, 1)
            dve.wait_ge(v_rooted, 1)
            link(nc.vector.tensor_scalar(v_norm[:], v_norm[:], 1e-30, None, ALU.max))
            link(nc.vector.tensor_scalar(v_pow[:].bitcast(I32), v_norm[:].bitcast(I32), 0x7F800000, None,
                                         ALU.bitwise_and))
            nc.vector.tensor_scalar(v_unscale[:], v_pow[:], 1.0 / V_LIMIT, None, ALU.mult)
            link(nc.vector.reciprocal(v_scale[:], v_pow[:]))
            link(nc.vector.tensor_scalar(v_scale[:], v_scale[:], V_LIMIT, None, ALU.mult))
            nc.vector.tensor_tensor(wv, wv, v_scale[:].unsqueeze(2).broadcast_to([P, NP, C]), ALU.mult
                                    ).then_inc(wv_scaled, 1)

            dve.wait_ge(a_in, 48)
            for w in (wkv, wkv_b):
                w8 = w.rearrange("p (h d) -> p h d", d=HD)
                link(nc.vector.tensor_reduce(wkv_mean[:, 0:32], w8, AX, ALU.add))
                link(nc.vector.scalar_tensor_tensor(w8, wkv_mean[:, 0:32].unsqueeze(2).broadcast_to([P, 32, HD]),
                                                    -1.0 / HD, w8, ALU.mult, ALU.add))
            for s in range(2):
                for dst, i in ((gamma, s), (beta, 2 + s)):
                    last = nc.vector.tensor_copy(dst[:, s * C:(s + 1) * C].rearrange("p (h d) -> p h d", d=HD),
                                                 gb8[:, i, :].unsqueeze(1).broadcast_to([P, C // HD, HD]))
            last.then_inc(gamma_ready, 1)
            dve.wait_ge(bias_in, 32)
            nc.vector.tensor_tensor(kv_bias.rearrange("p (h e) -> p h e", e=HD),
                                    mask.rearrange("p (h e) -> p h e", e=HD),
                                    kv_bias8.unsqueeze(1).broadcast_to([P, C // HD, HD]), ALU.mult)
            link(nc.vector.tensor_scalar(temp, temp, 1.0 / T, None, ALU.mult))
            layernorm(0)

            def kv_move(u):
                dve.wait_ge(kv_done, u + 1)
                nc.vector.tensor_tensor(kv[:, 4 * u:4 * u + 4, :],
                                        ps[:, 2 * u:2 * u + 2, :].rearrange("p b (t n) -> p (b t) n", n=256),
                                        wkv_b.unsqueeze(1).broadcast_to([P, 4, 256]), ALU.add
                                        ).then_inc(kv_moved, 1)

            def groups(u):
                return kv[:, 4 * u:4 * u + 4, :].rearrange("p t (h d) -> p (t h) d", d=HD)

            def kv_sum(u):
                dve.wait_ge(kv_squared, u + 1)
                nc.vector.tensor_reduce(kv_rstd[:, u, :], kv_sq[:, u % 2, :].rearrange("p (g d) -> p g d", d=HD),
                                        AX, ALU.add).then_inc(kv_summed, 1)

            def kv_norm(u):
                dve.wait_ge(kv_rooted, u + 1)
                link(nc.vector.reciprocal(kv_rstd[:, u, :], kv_rstd[:, u, :]))
                nc.vector.tensor_tensor(groups(u), groups(u),
                                        kv_rstd[:, u, :].unsqueeze(2).broadcast_to([P, 128, HD]), ALU.mult
                                        ).then_inc(kv_scaled, 1)

            kv_move(0)
            kv_move(1)
            kv_sum(0)
            kv_norm(0)
            kv_move(2)
            kv_move(3)
            for u in range(1, 4):
                kv_sum(u)
                kv_norm(u)
            dve.wait_ge(wv_turned, 1)
            nc.vector.tensor_copy(wvT.rearrange("p (b n) -> p b n", b=2), ps[:, 5:7, :])
            nc.vector.tensor_scalar(y_bias[:], ps[:, 7, 0:1], out_b[:], None, ALU.add).then_inc(wv_ready, 1)
            dve.wait_ge(kvprod_done, 1)
            link(nc.vector.scalar_tensor_tensor(kv_bd, ps[:, 4, 0:P], temp, mask, ALU.mult, ALU.mult))
            nc.vector.tensor_tensor(kv_bd, kv_bd, kv_bias, ALU.add).then_inc(kv_bd_ready, 1)

            def att_move(b):
                dve.wait_ge(att_done, b + 1)
                nc.vector.tensor_tensor(attT[:, cols(b)], ps[:, b, :], xnT[:, cols(b)], ALU.add).then_inc(att_moved, 1)

            def a_out(b):
                link(nc.vector.tensor_tensor(xT[:, cols(b)], xT[:, cols(b)], xnT[:, cols(b)], ALU.add))
                dve.wait_ge(p2_done, b + 1)
                nc.vector.scalar_tensor_tensor(xT[:, cols(b)], ps[:, b, :], p2b, xT[:, cols(b)], ALU.add, ALU.add
                                               ).then_inc(x_new, 1)

            for b in range(NB):
                att_move(b)
            for b in range(NB):
                a_out(b)

            layernorm(1)
            swiglu(0)
            layernorm(2)
            def take(job, bank, m, n):
                dve.wait_ge(aux_done, m + 1)
                src = ps[:, bank, :]
                kind, i = job[0], job[1]
                if kind == "proj":
                    b = job[2]
                    link(nc.vector.tensor_scalar(k1[i][:, cols(b)], src, bkq[i][:], None, ALU.add))
                    if b % 2:
                        nc.vector.scalar_tensor_tensor(q2[i][:, cols(b)], src, bkq[i][:], f32(k1[i][:, cols(b)]),
                                                       ALU.add, ALU.subtract).then_inc(aux_used, 1)
                        dve.wait_ge(aux_used, m + 1)
                        dve.sem_inc(kq_split)
                    else:
                        nc.vector.scalar_tensor_tensor(q2[i][:, cols(b)], src, bkq[i][:], f32(k1[i][:, cols(b)]),
                                                       ALU.add, ALU.subtract).then_inc(aux_used, 1)
                elif kind == "max":
                    t, kb = max_operands(job[2])
                    ins = nc.vector.tensor_reduce(maxes[:, t, kb:kb + 1], src, AX, ALU.max).then_inc(aux_used, 1)
                    if job[2] == 4 * NT - 1:
                        dve.wait_ge(aux_used, m + 1)
                        link(nc.vector.tensor_reduce(row_max[:], maxes[:], AX, ALU.max))
                        nc.vector.tensor_scalar(neg_max[:], row_max[:], -1.0, P_SCALE * DH ** 0.5, ALU.mult, ALU.add
                                                ).then_inc(neg_max_ready, 1)
                elif kind == "shift":
                    if not (isinstance(n, int) and n < 0):
                        dve.wait_ge(shift_in, n * 16 + 16)
                    nc.vector.tensor_copy(shift[:], src[0:NT, 0:P]).then_inc(aux_used, 1)
                    dve.wait_ge(aux_used, m + 1)
                    dve.sem_inc(shift_ready)
                elif kind == "turn":
                    nc.vector.tensor_scalar(oT[:], src, unscale[:], None, ALU.mult).then_inc(aux_used, 1)
                else:
                    nc.vector.tensor_tensor(xT[:, cols(job[1])], src, xT[:, cols(job[1])], ALU.add
                                            ).then_inc(aux_used, 1)

            dve.wait_ge(w_in[0], 32)
            for b in range(NB):
                take(("proj", 0, b), aux_bank(b, True), b, -1)
            link(nc.vector.tensor_scalar(xT[:], xT[:], y_bias[:], None, ALU.add))
            for n in range(4 * NT):
                take(("max", 0, n), aux_bank(NB + n, True), NB + n, -1)
            take(("shift", 0), aux_bank(NB + 4 * NT, True), NB + 4 * NT, -1)

            def low(g, p, last):
                c = g * PAIR + p
                dve.wait_ge(hi_done, c + 1)
                if not (isinstance(c, int) and c < RING):
                    dve.wait_ge(pv_done, c - RING + 1)
                nc.vector.tensor_tensor(p_lo[:, p % RING, :], p32[:, p % RING, :], p_hi[:, p % RING, :], ALU.subtract
                                        ).then_inc(lo_dve, 1)

            dve.sem_inc(o_used)

            def o_sum(g, q):
                dve.wait_ge(o_read, g * 8 + q // 8 + 1)
                nc.vector.reciprocal(rden[:].unsqueeze(3), o_raw[:, :, :, DH:DH + 1]).then_inc(dve_step, 1)
                nc.vector.tensor_tensor(o_raw[:, :, :, 0:DH], o_raw[:, :, :, 0:DH], o_raw[:, :, :, DH + 1:VW], ALU.add
                                        ).then_inc(dve_step, 1)
                steps["n"] += 2

            def o_divide(q):
                qb, i = q // 8 % 4, q // HEAD % 2
                dst = o_sb[:, 4 * qb:4 * qb + 4, i * DH:(i + 1) * DH].rearrange("p (b t) d -> p b t d", b=2)
                step_wait(0)
                nc.vector.tensor_tensor(dst, o_raw[:, :, :, 0:DH], rden[:].unsqueeze(3).broadcast_to([P, 2, 2, DH]),
                                        ALU.mult).then_inc(o_used, 1)

            def tick(g, p, last, first=False):
                jobs = first_jobs(p) if first else aux_jobs(p, last)
                done = aux_before(p, last, first)
                q = p - LAG - 1
                ends = q >= 0 and q % 8 == 7 and not (last and q >= PAIR)
                for k in range(3):
                    if k < len(jobs):
                        m = done + k if first else g * AUX_PAIR + done + k
                        take(jobs[k], aux_bank(done + k), m, g * 2 + p // HEAD)
                    if k == 0 and ends:
                        o_sum(g, q)
                    if k == 1 and ends:
                        o_divide(q)
                if p and low_on_dve((p - 1) % PAIR, last) and not (last and p - 1 >= PAIR):
                    low(g, p - 1, last)

            for p in range(ROT):
                tick(0, p, False, first=True)
            steps["per"] = 8 + 2 * 8 + 2
            with dve.Fori(0, NP - 1) as g:
                steps["g"], before = g, steps["n"]
                for p in range(ROT, ROT + PAIR):
                    tick(g, p, False)
                assert steps["n"] - before == steps["per"], steps["n"] - before
            steps["g"], steps["n"] = None, before + (NP - 1) * steps["per"]
            for p in range(ROT, ROT + PAIR):
                tick(NP - 1, p, True)

            layernorm(3)
            swiglu(1)

        @block.gpsimd
        def _(pool):
            for i in range(2):
                nc.gpsimd.memset(k2[i][0:DH, :].bitcast(F32), 0.0).then_inc(zeros_done, 1)
            for i in range(2):
                pool.wait_ge(zeros_done, i + 1)
                nc.gpsimd.memset(k2[i][0:1, :].bitcast(F32), 1.0).then_inc(ones_done, 1)
            for u in range(4):
                kv_u = kv[:, 4 * u:4 * u + 4, :]
                pool.wait_ge(kv_scaled, u + 1)
                nc.gpsimd.tensor_tensor(kv_u, kv_u, gamma.unsqueeze(1).broadcast_to([P, 4, 256]), ALU.mult
                                        ).then_inc(kv_gamma, 1)
                pool.wait_ge(kv_gamma, u + 1)
                nc.gpsimd.tensor_tensor(kv_u, kv_u, beta.unsqueeze(1).broadcast_to([P, 4, 256]), ALU.add
                                        ).then_inc(kv_ready, 1)
            pool.wait_ge(x_new, 2 * NB)
            nc.gpsimd.memset(v_all[:, :, :, DH:DH + 1], 1.0).then_inc(ones_done, 1)
            for i in range(2 * NT):
                t, half = divmod(i, 2)
                heads = slice(half * 8, half * 8 + 8)
                pool.wait_ge(v_moved, i + 1)
                nc.gpsimd.tensor_tensor(v_all[:, heads, t, DH + 1:VW],
                                        v32[:, i % 8, :].rearrange("p (h d) -> p h d", d=DH),
                                        v_all[:, heads, t, 0:DH], ALU.subtract).then_inc(v_lo_done, 1)

            def tick(g, p, last, first=False):
                if low_on_dve(p % PAIR, last):
                    return
                c = g * PAIR + p
                pool.wait_ge(hi_done, c + 1)
                if not (first and p < RING):
                    pool.wait_ge(pv_done, c - RING + 1)
                nc.gpsimd.tensor_tensor(p_lo[:, p % RING, :], p32[:, p % RING, :], p_hi[:, p % RING, :], ALU.subtract
                                        ).then_inc(lo_pool, 1)

            for p in range(ROT):
                tick(0, p, False, first=True)
            with pool.Fori(0, NP - 1) as g:
                for p in range(ROT, ROT + PAIR):
                    tick(g, p, False)
            for p in range(ROT, PAIR):
                tick(NP - 1, p, True)


def kernel(**inputs):
    import numpy as np
    import concourse.bacc as bacc
    from concourse.bass_utils import run_bass_kernel_spmd as run

    x = {k.replace("L0_", ""): np.asarray(v) for k, v in inputs.items()}
    C, T, H2, H = 128, x["attn_a_x"].shape[1], 16, 16
    W, bW = x["attn_b_W_w"], x["attn_b_W_b"]
    D = H2 * DH
    by_head = lambda w: w.reshape(H2, DH, *w.shape[1:])
    eye = np.eye(C, dtype=np.float32)
    first_row = np.zeros((C, C), np.float32)
    first_row[::32] = 1.0
    arrays = {
        "xT": x["attn_a_x"][0].T,
        "w_a": np.concatenate([x["attn_a_qkv_w"][C:], x["attn_a_qkv_w"][:C], x["attn_a_p1_w"], x["attn_a_p2_w"]]).T,
        "rows": np.concatenate([x["attn_a_kn_g"], x["attn_a_vn_g"], x["attn_a_kn_b"], x["attn_a_vn_b"],
                                x["attn_a_qkv_b"][C:]]),
        "columns": np.concatenate([
            np.stack([x["attn_a_qkv_b"][:C], x["attn_a_p1_b"], x["attn_a_p2_b"], x["attn_b_out_b"],
                      np.repeat(x["attn_a_temperature"].reshape(-1), C // H)], axis=1),
            x["attn_a_attn_bias"].reshape(C, C // H), bW[2 * D:].reshape(D // C, C).T], axis=1),
        "wkq": np.concatenate([by_head(W[D:2 * D]), by_head(W[0:D])], axis=1).transpose(0, 2, 1),
        "bkq": np.concatenate([by_head(bW[D:2 * D]), by_head(bW[0:D])], axis=1),
        "wv": W[2 * D:], "woT": x["attn_b_out_w"].T,
        "wgu": np.concatenate([x["ffn_w_gate"], x["ffn_w_up"]]).reshape(-1, C, C).transpose(2, 0, 1),
        "wd": x["ffn_w_down"].T,
        "consts": np.stack([eye, eye - np.float32(1.0 / C), np.full((C, C), 1.0 / C, np.float32), first_row], axis=1),
        "mask": np.kron(np.eye(H, dtype=np.float32), np.ones((C // H, C // H), np.float32)),
    }
    nc = bacc.Bacc("TRN2", target_bir_lowering=False, num_devices=1)
    maps, args = {}, {}
    for name, v in arrays.items():
        v = np.ascontiguousarray(v)
        maps[f"in_{name}"] = v
        args[name] = nc.dram_tensor(f"in_{name}", v.shape, mybir.dt.from_np(v.dtype), kind="ExternalInput").ap()
    args["out"] = nc.dram_tensor("out_xT", (C, T), F32, kind="ExternalOutput").ap()
    block_program(nc, args)
    r = run(nc, [maps], core_ids=[0])
    return np.ascontiguousarray(np.asarray(r.results[0]["out_xT"]).T).reshape(1, T, C)
```

```python
import math
from contextlib import ExitStack

import concourse.bass as bass
from concourse import mybir

F32 = mybir.dt.float32
F32R = mybir.dt.float32r
F16 = mybir.dt.float16
I32 = mybir.dt.int32
ALU = mybir.AluOpType
ACT = mybir.ActivationFunctionType
AX = mybir.AxisListType.X

P = 128
EPS = 1e-5
BLK = 512
DH = 64
HD = 8
VW = 2 * DH + 1
LAG = 3
RING = 4
P_SCALE = math.log(32.0)
V_LIMIT = 2.0 ** 13

PAIR = 64
HEAD = 32
ROT = 6
MAX_FROM = 5
SIDE = 3
SHIFT_AT = 29
H_RING = 5
DOWN_BANK = (0, 1, 0, 3)
LOW_DVE = (2, 29)


def aux_jobs(p, last):
    v, parity = p % HEAD, (p // HEAD + 1) % 2
    jobs = []
    for b in range(4):
        if p % PAIR == (HEAD + 8 * b + 12) % PAIR:
            jobs.append(("turn", b))
        if p % PAIR == (HEAD + 8 * b + 13) % PAIR:
            jobs.append(("out", b))
    if last and p >= HEAD:
        return jobs
    if v < 2:
        jobs += [("proj", parity, 2 * v), ("proj", parity, 2 * v + 1)]
    if MAX_FROM <= v < SHIFT_AT:
        n = sum(SIDE - len(aux_jobs(p - v + u + PAIR, True)) for u in range(MAX_FROM, v))
        jobs = [("max", parity, k) for k in range(n, min(64, n + SIDE - len(jobs)))] + jobs
    if v == SHIFT_AT:
        jobs.append(("shift", parity))
    return jobs


def max_operands(n):
    return (n // 2, n % 2) if n < 16 else (8 + (n - 16) // 2, n % 2) if n < 32 else ((n - 32) // 2, 2 + n % 2)


def low_on_dve(p, last):
    if last and HEAD <= p:
        return p % 3 == 1
    return p % HEAD in LOW_DVE


def block_program(nc, a):
    T = a["xT"].shape[1]
    C = P
    NT, NB = T // P, T // BLK
    H2 = a["wkq"].shape[0]
    NP = H2 // 2
    FH = a["wd"].shape[0] // P
    assert T == 2048 and a["xT"].shape[0] == C and H2 * DH == 1024 and FH == 3

    with ExitStack() as ctx:
        def sb(name, shape, dt=F32):
            return ctx.enter_context(nc.sbuf_tensor(name, shape, dt))

        def sem(name):
            return ctx.enter_context(nc.semaphore(name))

        ps = ctx.enter_context(nc.psum_tensor("ps", [P, 8, BLK], F32))
        s_ps = ps[:, 0:4, :].rearrange("p (r k) n -> p r k n", r=2)
        o_ps = ps[:, 4:6, :]
        def aux_bank(m, first=False):
            return 4 + m % 4 if first else 6 + m % 2


        xT = sb("xT_sb", [P, T])
        xn_hi, xn_lo = (sb(n, [P, T], F32R) for n in ("xn_hi", "xn_lo"))
        consts = sb("consts", [P, 4, P])
        ident, centre, mean, first_row = (consts[:, i, :] for i in range(4))
        columns = sb("columns", [P, 5 + HD + 8])
        bq, p1b, p2b, out_b, temp = (columns[:, i:i + 1] for i in range(5))
        kv_bias8, v_bias = columns[:, 5:5 + HD], columns[:, 5 + HD:]
        eps = sb("eps", [P, 1])
        k1 = [sb(f"k1_{i}", [P, T], F32R) for i in range(2)]
        k2 = [sb(f"k2_{i}", [P, T], F32R) for i in range(2)]
        q1 = [sb(f"q1_{i}", [P, T], F32R) for i in range(2)]
        q2 = [sb(f"q2_{i}", [P, T], F32R) for i in range(2)]
        v_flat = sb("v_all", [P, H2 * NT * VW], F16)
        v_all = v_flat[:].rearrange("p (h t v) -> p h t v", h=H2, t=NT)
        v_head = [sb(f"v_head{i}", [P, NT, VW], F16) for i in range(2)]
        wkq = sb("wkq", [P, P])
        wkq_hi, wkq_lo = sb("wkq_hi", [P, P], F32R), sb("wkq_lo", [P, P], F32R)
        bkq = [sb(f"bkq{i}", [P, 1]) for i in range(2)]
        wo = sb("wo_pair", [P, C])
        unscale = sb("unscale", [P, 1])
        p32 = sb("p32", [P, RING, 2 * BLK])
        p_hi = sb("p_hi", [P, RING, 2 * BLK], F16)
        p_lo = sb("p_lo", [P, RING, 2 * BLK], F16)
        maxes = sb("maxes", [P, NT, NB])
        row_max = sb("row_max", [P, NT])
        neg_max = sb("neg_max", [P, NT])
        shift = sb("shift", [NT, P], F32R)
        rden = sb("rden", [P, 2, 2])
        o_raw = sb("o_raw", [P, 2, 2, VW])
        oT = o_raw[:].rearrange("p b t v -> p (b t v)")[:, 0:BLK]
        o_sb = sb("o_sb", [P, NT, 2 * DH])
        v_unscale = sb("v_unscale", [P, NP])
        y_bias = sb("y_bias", [P, 1])
        idle = sb("idle", [P, 1])

        room = v_flat[:].bitcast(F32)
        at = [0]

        def carve(n):
            at[0] += n
            assert at[0] <= room.shape[1]
            return room[:, at[0] - n:at[0]]

        kv = carve(NT * 256).rearrange("p (t n) -> p t n", n=256)
        kv_sq = carve(2048).rearrange("p (r n) -> p r n", r=2)
        qT, attT, hT = carve(T), carve(T), carve(T)
        w_a = carve(5 * P)
        rows = carve(4 * HD + 256)
        gb8 = rows[:, 0:4 * HD].rearrange("p (s n) -> p s n", n=HD)
        wkv, wkv_b = w_a[:, 0:256], rows[:, 4 * HD:]
        wq, p1w, p2w = (w_a[:, 256 + i * P:256 + (i + 1) * P] for i in range(3))
        wkv_mean = carve(64)
        mask = carve(P)
        gamma, beta = carve(256), carve(256)
        kv_rstd = carve(4 * 128).rearrange("p (u n) -> p u n", u=4)
        kv_bd, kv_bias = carve(P), carve(P)
        ff_w = carve(3 * FH * P)
        v_norm, v_pow, v_scale = carve(NP), carve(NP), carve(NP)
        ff_s, ff_h = (room[:, i * BLK:(i + 3) * BLK].rearrange("p (r n) -> p r n", r=3) for i in (0, 3))
        wv = p_hi[:].rearrange("p r n -> p (r n)").bitcast(F32)[:, 0:1024].rearrange("p (j c) -> p j c", c=C)
        wv_sq = p_hi[:].rearrange("p r n -> p (r n)").bitcast(F32)[:, 1024:2048].rearrange("p (j c) -> p j c", c=C)
        ints, w32 = (ff_w.bitcast(t).rearrange("p (j c) -> p j c", c=P) for t in (I32, F32))
        w_hi, w_lo = (w[:, 0:3 * FH * P].rearrange("p (j c) -> p j c", c=P) for w in (k1[0], q1[0]))

        def h_parts(i):
            r = i % H_RING
            if r == 4:
                return k1[0][:, 3 * BLK:], q1[0][:, 3 * BLK:]
            return k2[0][:, r * BLK:(r + 1) * BLK], q2[0][:, r * BLK:(r + 1) * BLK]

        wv_hi, wv_lo = q2[1][:, 0:2 * BLK], q2[1][:, 2 * BLK:4 * BLK]
        woT = p_lo[:].rearrange("p r n -> p (r n)").bitcast(F32)[:, 0:1024].rearrange("p (j c) -> p j c", c=C)
        xnT = o_sb[:].rearrange("p t n -> p (t n)")
        ln_sq = p32[:, :, 0:BLK]
        ln_std = p32[:, 0, BLK:2 * BLK]
        v32 = p32[:].rearrange("p r n -> p (r n)").rearrange("p (s n) -> p s n", n=BLK)

        def f32(ap):
            return ap.bitcast(F32)

        x_in = [sem(f"x_in{b}") for b in range(NB)]
        const_in, a_in, ff_in, vw_in, bias_in = (
            sem(n) for n in ("const_in", "a_in", "ff_in", "vw_in", "bias_in"))
        dve_step = sem("dve_step")
        centred, squared, averaged, rooted, inverted, spread_std, normed = (
            sem(n) for n in ("centred", "squared", "averaged", "rooted", "inverted", "spread_std", "normed"))
        kv_done, kv_moved, kv_squared, kv_summed, kv_rooted, kv_scaled, kv_gamma, kv_ready = (
            sem(n) for n in ("kv_done", "kv_moved", "kv_squared", "kv_summed", "kv_rooted", "kv_scaled",
                             "kv_gamma", "kv_ready"))
        last_kv_ready = sem("last_kv_ready")
        zeros_done, eps_ready = sem("zeros_done"), sem("eps_ready")
        gamma_ready, q_done, q_moved, kvprod_done, kv_bd_ready = (
            sem(n) for n in ("gamma_ready", "q_done", "q_moved", "kvprod_done", "kv_bd_ready"))
        att_done, att_moved, p1_done, gelu_done, p2_done, x_new = (
            sem(n) for n in ("att_done", "att_moved", "p1_done", "gelu_done", "p2_done", "x_new"))
        w32_ready, w_hi_ready, w_lo_ready, gu_done, silu_done, h_done, h_hi_done, h_lo_done, down_done = (
            sem(n) for n in ("w32_ready", "w_hi_ready", "w_lo_ready", "gu_done", "silu_done", "h_done", "h_hi_done", "h_lo_done",
                             "down_done"))
        xn_hi_done, xn_lo_done = sem("xn_hi_done"), sem("xn_lo_done")
        v_summed, v_rooted, wv_scaled, wv_turned, wv_ready, v_done, v_moved, v_lo_done, ones_done = (
            sem(n) for n in ("v_summed", "v_rooted", "wv_scaled", "wv_turned", "wv_ready", "v_done",
                             "v_moved", "v_lo_done", "ones_done"))
        w_in = [sem(f"w_in{i}") for i in range(2)]
        wkq_ready = sem("wkq_ready")
        v_in = [sem(f"v_in{i}") for i in range(2)]
        wo_in = sem("wo_in")
        kq_split = sem("kq_split")
        spread_hi = sem("spread_hi")
        spread_lo = [sem(f"spread_lo{i}") for i in range(2)]
        shift_ready, shift_in = sem("shift_ready"), sem("shift_in")
        neg_max_ready = sem("neg_max_ready")
        aux_done, aux_used = sem("aux_done"), sem("aux_used")
        scores_done = sem("scores_done")
        hi_done = sem("hi_done")
        lo_pool, lo_dve = sem("lo_pool"), sem("lo_dve")
        pv_done, o_read, o_used = sem("pv_done"), sem("o_read"), sem("o_used")
        stored = sem("stored")

        AUX_PAIR = sum(len(aux_jobs(p, False)) for p in range(ROT, ROT + PAIR))
        def first_jobs(p):
            return [j for j in aux_jobs(p, False) if j[0] in ("proj", "max", "shift")]

        PROLOGUE = [j for p in range(ROT) for j in first_jobs(p)]
        AUX_FIRST = NB + 4 * NT + 1
        assert AUX_PAIR % 2 == 0

        def aux_before(p, last, first=False):
            if first:
                return AUX_FIRST + sum(len(first_jobs(q)) for q in range(p))
            return AUX_FIRST + len(PROLOGUE) + sum(len(aux_jobs(q, last)) for q in range(ROT, p))

        def low_count(p, last, dve):
            return sum(low_on_dve(q % PAIR, last) == dve for q in range(p + 1))

        LOW_PAIR = {dve: low_count(PAIR - 1, False, dve) for dve in (True, False)}

        block = ctx.enter_context(nc.Block())

        @block.sync
        def _(sp):
            for b in range(NB):
                sp.dma_start(xT[:, b * BLK:(b + 1) * BLK], a["xT"][:, b * BLK:(b + 1) * BLK]).then_inc(x_in[b], 16)
            sp.dma_start(w_a, a["w_a"]).then_inc(a_in, 16)
            sp.dma_start(rows, a["rows"].rearrange("(o n) -> o n", o=1).broadcast_to([P, 4 * HD + 256])
                         ).then_inc(a_in, 16)
            sp.dma_start(mask, a["mask"]).then_inc(a_in, 16)

            def load_ff():
                sp.dma_start(ints[:, 0:2 * FH, :], a["wgu"]).then_inc(ff_in, 16)
                sp.dma_start(ints[:, 2 * FH:3 * FH, :], a["wd"].rearrange("(j p) d -> p j d", p=P)).then_inc(ff_in, 16)

            load_ff()

            def load_w(i, n):
                if not isinstance(n, int) or n:
                    sp.wait_ge(wkq_ready, n)
                sp.dma_start(wkq[:], a["wkq"][bass.ds(n, 1), :, :].rearrange("o c m -> (o c) m")
                             ).then_inc(w_in[i], 16)
                sp.dma_start(bkq[i][:], a["bkq"][bass.ds(n, 1), :].rearrange("o (m u) -> (o m) u", u=1)
                             ).then_inc(w_in[i], 16)

            def load_v(i, n):
                sp.dma_start(v_head[i][:].rearrange("p t v -> p (t v)"),
                             v_all[:, bass.ds(n, 1), :, :].rearrange("p o t v -> p (o t v)")).then_inc(v_in[i], 16)

            def load_wo(g):
                sp.dma_start(wo[:], a["woT"][bass.ds(g * P, P), :]).then_inc(wo_in, 16)
                sp.dma_start(unscale[:], v_unscale[:, bass.ds(g, 1)]).then_inc(wo_in, 16)

            def spread(i, n, half):
                cols = slice(half * T // 2, (half + 1) * T // 2)
                sp.wait_ge(kq_split, n * 2 + half + 1)
                sp.dma_start(f32(q1[i][0:DH, cols]), f32(k1[i][DH:P, cols])).then_inc(spread_hi, 16)
                sp.dma_start(f32(q1[i][DH:P, cols]), f32(k1[i][DH:P, cols])).then_inc(spread_hi, 16)
                sp.dma_start(f32(k2[i][DH:P, cols]), f32(k1[i][0:DH, cols])).then_inc(spread_hi, 16)
                sp.wait_ge(spread_hi, n * 96 + half * 48 + 48)
                sp.dma_start(f32(k1[i][DH:P, cols]), f32(q2[i][0:DH, cols])).then_inc(spread_lo[half], 16)

            def place_shift(i, n):
                sp.wait_ge(shift_ready, n + 1)
                for half in range(2):
                    sp.wait_ge(spread_lo[half], n * 16 + 16)
                sp.dma_start(f32(q2[i][0:1, :]).rearrange("o (t n) -> o t n", t=NT), f32(shift[:])).then_inc(shift_in, 16)

            load_w(0, 0)
            load_w(1, 1)
            for half in range(2):
                spread(0, 0, half)
            place_shift(0, 0)
            sp.wait_ge(v_lo_done, 2 * NT)
            sp.wait_ge(ones_done, 3)
            load_v(0, 0)
            load_v(1, 1)
            load_wo(0)
            for half in range(2):
                spread(1, 1, half)

            def pair_moves(g, last):
                if not last:
                    load_w(0, g * 2 + 2)
                place_shift(1, g * 2 + 1)
                if last:
                    for i in range(2):
                        sp.wait_ge(v_in[i], NP * 16)
                    load_ff()
                    return
                for half in range(2):
                    spread(0, g * 2 + 2, half)
                load_w(1, g * 2 + 3)
                sp.wait_ge(pv_done, g * PAIR + HEAD)
                load_v(0, g * 2 + 2)
                place_shift(0, g * 2 + 2)
                for half in range(2):
                    spread(1, g * 2 + 3, half)
                sp.wait_ge(pv_done, g * PAIR + PAIR)
                load_v(1, g * 2 + 3)
                sp.wait_ge(aux_used, g * AUX_PAIR + aux_before(ROT + PAIR, False))
                load_wo(g + 1)

            with sp.Fori(0, NP - 1) as g:
                pair_moves(g, False)
            pair_moves(NP - 1, True)
            for b in range(NB):
                sp.wait_ge(x_new, 2 * NB + b + 1)
                sp.dma_start(a["out"][:, b * BLK:(b + 1) * BLK], xT[:, b * BLK:(b + 1) * BLK]).then_inc(stored, 16)
            sp.wait_ge(stored, 16 * NB)

        @block.tensor
        def _(pe):
            def cols(b):
                return slice(b * BLK, (b + 1) * BLK)

            def keep_warm(n, bank):
                for _ in range(n):
                    pe.matmul(ps[:, bank, :], centre, xT[:, cols(0)], start=True, stop=True)

            def layernorm(k, x_ready):
                def average(b):
                    pe.wait_ge(squared, NB * k + b + 1)
                    pe.matmul(ps[32 * b:32 * b + 32, 7, :], mean[:, 0:32], ln_sq[:, b, :], start=True, stop=True
                              ).then_inc(averaged, 1)

                for b in range(NB):
                    pe.wait_ge(*x_ready(b))
                    pe.matmul(ps[:, b, :], centre, xT[:, cols(b)], start=True, stop=True).then_inc(centred, 1)
                    if b:
                        average(b - 1)
                average(NB - 1)
                keep_warm(5, 4)
                pe.wait_ge(inverted, k + 1)
                for b in range(NB):
                    pe.matmul(ps[:, 4 + b, :], first_row[32 * b:32 * b + 32, :], ln_std[32 * b:32 * b + 32, :],
                              start=True, stop=True).then_inc(spread_std, 1)

            def product(out, a_hi, a_lo, b_hi, b_lo, start=True, stop=True):
                pe.matmul(out, a_hi, b_hi, start=start, stop=False)
                pe.matmul(out, a_lo, b_hi, start=False, stop=False)
                return pe.matmul(out, a_hi, b_lo, start=False, stop=stop)

            def swiglu(f, k):
                n = NB * FH

                def down(b):
                    if b == 2:
                        pe.wait_ge(x_new, NB * (f + 1) + 1)
                    for j in range(FH):
                        if b == NB - 1 and j:
                            keep_warm(1, 2)
                        pe.wait_ge(h_lo_done, n * f + FH * b + j + 1)
                        w = 2 * FH + j
                        last = product(ps[:, DOWN_BANK[b], :], w_hi[:, w, :], w_lo[:, w, :], *h_parts(FH * b + j),
                                       start=(j == 0), stop=(j == FH - 1))
                    last.then_inc(down_done, 1)

                pe.wait_ge(w_lo_ready, f + 1)
                for i in range(n):
                    b, j = divmod(i, FH)
                    if j == 0:
                        pe.wait_ge(xn_lo_done, NB * (k - 1) + b + 1)
                    if i in (1, 2):
                        pe.wait_ge(normed, NB * k + 2 * i)
                    if i >= 3:
                        pe.wait_ge(h_done, n * f + i - 2)
                    bank = 2 + 2 * (i % 3)
                    product(ps[:, bank, :], w_hi[:, j, :], w_lo[:, j, :], xn_hi[:, cols(b)], xn_lo[:, cols(b)])
                    product(ps[:, bank + 1, :], w_hi[:, FH + j, :], w_lo[:, FH + j, :], xn_hi[:, cols(b)],
                            xn_lo[:, cols(b)]).then_inc(gu_done, 1)
                    if j == 1 and b:
                        down(b - 1)
                down(NB - 1)

            pe.wait_ge(const_in, 16)
            layernorm(0, lambda b: (x_in[b], 16))
            pe.wait_ge(gamma_ready, 1)
            for u in range(4):
                pe.wait_ge(normed, 2 if u == 0 else NB)
                for t in range(4 * u, 4 * u + 4):
                    last = pe.matmul(ps[:, t // 2, (t % 2) * 256:(t % 2) * 256 + 256], xnT[:, t * P:(t + 1) * P],
                                     wkv, start=True, stop=True, skip_group_check=True)
                last.then_inc(kv_done, 1)
            for b in range(NB):
                pe.wait_ge(kv_moved, b // 2 + 1)
                pe.matmul(ps[:, b, :], wq, xnT[:, cols(b)], start=True, stop=True).then_inc(q_done, 1)
            pe.wait_ge(kv_moved, 4)
            pe.wait_ge(wv_scaled, 1)
            for j in range(NP):
                pe.transpose(ps[:, 5 + j // 4, (j % 4) * P:(j % 4 + 1) * P], wv[:, j, :], ident)
            pe.wait_ge(bias_in, 32)
            for j in range(NP):
                last = pe.matmul(ps[:, 7, 0:1], woT[:, j, :], v_bias[:, j:j + 1], start=(j == 0), stop=(j == NP - 1))
            last.then_inc(wv_turned, 1)
            pe.wait_ge(q_moved, 1)
            for t in range(NT):
                if t == NT // 4:
                    keep_warm(1, 0)
                if t == NT // 2:
                    keep_warm(2, 0)
                if t < NT - 4:
                    pe.wait_ge(kv_ready, t // 4 + 1)
                else:
                    pe.wait_ge(last_kv_ready, 1)
                last = pe.matmul(ps[:, 4, 0:P], kv[:, t, 0:P], kv[:, t, P:2 * P], start=(t == 0), stop=(t == NT - 1))
            last.then_inc(kvprod_done, 1)
            keep_warm(2, 0)
            pe.wait_ge(kv_bd_ready, 1)
            pe.wait_ge(wv_ready, 1)
            for s in range(NB + 2):
                if s < NB:
                    pe.wait_ge(q_moved, s + 1)
                    pe.matmul(ps[:, s, :], kv_bd, qT[:, cols(s)], start=True, stop=True).then_inc(att_done, 1)
                if 1 <= s <= NB:
                    pe.wait_ge(att_moved, s)
                    pe.matmul(ps[:, 3 + s, :], p1w, attT[:, cols(s - 1)], start=True, stop=True).then_inc(p1_done, 1)
                if s >= 2:
                    pe.wait_ge(gelu_done, s - 1)
                    pe.matmul(ps[:, s - 2, :], p2w, hT[:, cols(s - 2)], start=True, stop=True).then_inc(p2_done, 1)

            layernorm(1, lambda b: (x_new, b + 1))
            swiglu(0, 1)
            layernorm(2, lambda b: (x_new, NB + max(b + 1, 3)))

            def aux(job, bank):
                out = ps[:, bank, :]
                kind, i = job[0], job[1]
                if kind == "proj":
                    c = cols(job[2])
                    return product(out, wkq_hi[:], wkq_lo[:], xn_hi[:, c], xn_lo[:, c])
                if kind == "max":
                    t, kb = max_operands(job[2])
                    return pe.matmul(out, q1[i][:, t * P:(t + 1) * P], k1[i][:, cols(kb)], start=True, stop=True)
                if kind == "shift":
                    return pe.transpose(out[0:NT, 0:P], neg_max[:], ident)
                if kind == "turn":
                    for t in range(4):
                        last = pe.transpose(out[:, t * P:(t + 1) * P], o_sb[:, 4 * i + t, :], ident)
                    return last
                return pe.matmul(out, wo[:], oT, start=True, stop=True)

            def scores(p, kt):
                i, (qb, kp) = p // HEAD % 2, divmod(p % HEAD, 8)
                k = slice((2 * kp + kt) * P, (2 * kp + kt + 1) * P)
                out = s_ps[:, p % 2, kt, :]
                pe.matmul(out, k1[i][:, k], q1[i][:, cols(qb)], start=True, stop=False)
                last = pe.matmul(out, k2[i][:, k], q2[i][:, cols(qb)], start=False, stop=True)
                if kt == 1:
                    last.then_inc(scores_done, 1)

            def times_v(p):
                i, v = p // HEAD % 2, p % HEAD
                for kt in range(2):
                    k = 2 * (v % 8) + kt
                    for t in range(4):
                        at0 = (t % 2) * VW
                        w = slice(kt * BLK + t * P, kt * BLK + (t + 1) * P)
                        pe.matmul(o_ps[:, t // 2, at0:at0 + VW], p_hi[:, p % RING, w], v_head[i][:, k, :],
                                  start=(k == 0 and t % 2 == 0), stop=False, skip_group_check=True)
                        last = pe.matmul(o_ps[:, t // 2, at0:at0 + DH + 1], p_lo[:, p % RING, w],
                                         v_head[i][:, k, 0:DH + 1], start=False, stop=(k == NT - 1),
                                         skip_group_check=True)
                last.then_inc(pv_done, 1)

            pe.wait_ge(normed, 3 * NB)
            pe.wait_ge(wkq_ready, 1)
            for b in range(NB):
                pe.wait_ge(xn_lo_done, NB + b + 1)
                aux(("proj", 0, b), aux_bank(b, True)).then_inc(aux_done, 1)

            def first_max(n):
                if n == 0:
                    pe.wait_ge(spread_lo[0], 16)
                if n == 16:
                    pe.wait_ge(spread_lo[1], 16)
                pe.wait_ge(aux_used, NB + n - 3)
                aux(("max", 0, n), aux_bank(NB + n, True)).then_inc(aux_done, 1)

            AHEAD, WITH = 6, 3
            for i in range(2 * NT):
                t, half = divmod(i, 2)
                if i >= 4:
                    pe.wait_ge(v_moved, i - 3)
                tile, w = slice(t * P, (t + 1) * P), slice(half * BLK, (half + 1) * BLK)
                product(ps[:, i % 4, :], xn_hi[:, tile], xn_lo[:, tile], wv_hi[:, w], wv_lo[:, w]).then_inc(v_done, 1)
                n = WITH * (i - AHEAD)
                for k in range(max(n, 0), min(n + WITH, 4 * NT)):
                    first_max(k)
                if n - WITH < 4 * NT <= n:
                    pe.wait_ge(neg_max_ready, 1)
                    aux(("shift", 0), aux_bank(NB + 4 * NT, True)).then_inc(aux_done, 1)

            def tick(g, p, last, first=False):
                c = g * PAIR + p
                n = g * 2 + p // HEAD
                jobs = first_jobs(p) if first else aux_jobs(p, last)
                done = aux_before(p, last, first)

                def side(k):
                    if k < 0:
                        return
                    job, m = jobs[k], done + k if first else g * AUX_PAIR + done + k
                    if job[0] == "proj" and job[2] == 0:
                        pe.wait_ge(wkq_ready, n + 2)
                    for half in range(2):
                        if job[0] == "max" and job[2] == 16 * half:
                            pe.wait_ge(spread_lo[half], (n + 1) * 16 + 16)
                    if job[0] == "shift":
                        pe.wait_ge(neg_max_ready, n + 2)
                    if job[0] == "turn":
                        pe.wait_ge(o_used, g * 8 + 6 + job[1])
                    if job[0] == "out" and job[1] == 0:
                        pe.wait_ge(wo_in, g * 32 + 32)
                    after_turn = job[0] == "out" and k == 0 and len(jobs) < 3
                    pe.wait_ge(aux_used, m if after_turn else m - 1)
                    aux(job, aux_bank(done + k)).then_inc(aux_done, 1)

                first_side = len(jobs) - 3
                side(first_side)
                if not (last and p >= PAIR):
                    if p % HEAD == 0:
                        pe.wait_ge(shift_in, n * 16 + 16)
                    if first and p < 2:
                        pe.wait_ge(v_moved, 2 * NT)
                    else:
                        pe.wait_ge(hi_done, c - 1)
                    scores(p, 0)
                    side(first_side + 1)
                    scores(p, 1)
                else:
                    side(first_side + 1)
                side(first_side + 2)
                q = p - LAG
                with_v = not (first and q < 0) and not (last and q >= PAIR)
                if with_v:
                    if q % HEAD == 0:
                        pe.wait_ge(v_in[q // HEAD % 2], (g + q // PAIR) * 16 + 16)
                    if q % 8 == 0 and not (first and q == 0):
                        pe.wait_ge(o_read, g * 8 + q // 8)
                    owner = low_on_dve(q % PAIR, last)
                    pe.wait_ge(lo_dve if owner else lo_pool, g * LOW_PAIR[owner] + low_count(q, last, owner))
                    times_v(q)
                assert len(jobs) <= 3

            for p in range(ROT):
                tick(0, p, False, first=True)
            with pe.Fori(0, NP - 1) as g:
                for p in range(ROT, ROT + PAIR):
                    tick(g, p, False)
            for p in range(ROT, ROT + PAIR):
                tick(NP - 1, p, True)

            layernorm(3, lambda b: (aux_used, (NP - 1) * AUX_PAIR + aux_before(ROT + PAIR, True)))
            swiglu(1, 3)

        @block.scalar
        def _(act):
            act.dma_start(consts[:], a["consts"]).then_inc(const_in, 16)
            act.dma_start(wv, a["wv"].rearrange("(j p) c -> p j c", p=P)).then_inc(vw_in, 16)
            act.dma_start(columns[:], a["columns"]).then_inc(bias_in, 16)
            act.dma_start(woT, a["woT"].rearrange("(j p) d -> p j d", p=P)).then_inc(bias_in, 16)

            def cols(b):
                return slice(b * BLK, (b + 1) * BLK)

            def load_table(f):
                nc.scalar.activation(idle[:], eps[:], f)

            def layernorm(k):
                if k:
                    load_table(ACT.Sqrt)
                for b in range(NB):
                    act.wait_ge(centred, NB * k + b + 1)
                    nc.scalar.activation(ln_sq[:, b, :], ps[:, b, :], ACT.Square).then_inc(squared, 1)
                act.wait_ge(averaged, NB * k + NB)
                if k == 0:
                    act.wait_ge(eps_ready, 1)
                nc.scalar.activation(ln_std, ps[:, 7, :], ACT.Sqrt, bias=eps[:]).then_inc(rooted, 1)
                for b in range(NB) if k else ():
                    act.wait_ge(normed, NB * k + b + 1)
                    nc.scalar.activation(xn_hi[:, cols(b)], xnT[:, cols(b)], ACT.Copy).then_inc(xn_hi_done, 1)

            def swiglu(f):
                n = NB * FH
                for i in range(n + 1):
                    if i < n:
                        act.wait_ge(gu_done, n * f + i + 1)
                        if i >= 3:
                            act.wait_ge(h_done, n * f + i - 2)
                        nc.scalar.activation(ff_s[:, i % 3, :], ps[:, 2 + 2 * (i % 3), :], ACT.Silu
                                             ).then_inc(silu_done, 1)
                    if i >= 1:
                        act.wait_ge(h_done, n * f + i)
                        if i > H_RING:
                            act.wait_ge(down_done, NB * f + (i - 1 - H_RING) // FH + 1)
                        nc.scalar.activation(h_parts(i - 1)[0], ff_h[:, (i - 1) % 3, :], ACT.Copy
                                             ).then_inc(h_hi_done, 1)

            act.wait_ge(v_summed, 1)
            nc.scalar.activation(v_norm, v_norm, ACT.Sqrt, scale=float(C)).then_inc(v_rooted, 1)

            layernorm(0)
            for u in range(4):
                act.wait_ge(kv_moved, u + 1)
                if u >= 2:
                    act.wait_ge(kv_summed, u - 1)
                nc.scalar.activation(kv_sq[:, u % 2, :], kv[:, 4 * u:4 * u + 4, :].rearrange("p t n -> p (t n)"),
                                     ACT.Square).then_inc(kv_squared, 1)
                act.wait_ge(q_done, u + 1)
                nc.scalar.activation(qT[:, cols(u)], ps[:, u, :], ACT.Identity, bias=bq).then_inc(q_moved, 1)
                act.wait_ge(kv_summed, u + 1)
                nc.scalar.activation(kv_rstd[:, u, :], kv_rstd[:, u, :], ACT.Sqrt, bias=eps[:], scale=1.0 / HD
                                     ).then_inc(kv_rooted, 1)
            for b in range(NB):
                act.wait_ge(p1_done, b + 1)
                nc.scalar.activation(hT[:, cols(b)], ps[:, 4 + b, :], ACT.Gelu, bias=p1b).then_inc(gelu_done, 1)

            layernorm(1)
            swiglu(0)
            layernorm(2)

            act.wait_ge(normed, 3 * NB)
            for i in range(2 * NT):
                t, half = divmod(i, 2)
                act.wait_ge(v_done, i + 1)
                nc.scalar.activation(v_all[:, half * 8:half * 8 + 8, t, 0:DH],
                                     ps[:, i % 4, :].rearrange("p (h d) -> p h d", d=DH), ACT.Copy)
                if i >= 8:
                    act.wait_ge(v_lo_done, i - 7)
                nc.scalar.activation(v32[:, i % 8, :], ps[:, i % 4, :], ACT.Copy).then_inc(v_moved, 1)

            def tick(g, p, last, first=False):
                c = g * PAIR + p
                q = p - LAG
                if not (last and p >= PAIR):
                    src = s_ps[:, p % 2, :, :].rearrange("p k n -> p (k n)")
                    act.wait_ge(scores_done, c + 1)
                    if not (first and p < RING):
                        r = p - RING
                        owner = low_on_dve(r % PAIR, last)
                        act.wait_ge(lo_dve if owner else lo_pool, g * LOW_PAIR[owner] + low_count(r, last, owner))
                    nc.scalar.activation(p32[:, p % RING, :], src, ACT.Exp, scale=DH ** -0.5)
                if q >= 0 and q % 8 == 7 and not (last and q >= PAIR):
                    act.wait_ge(pv_done, g * PAIR + q + 1)
                    act.wait_ge(o_used, g * 8 + q // 8 + 1)
                    nc.scalar.activation(o_raw[:], o_ps[:, :, 0:2 * VW].rearrange("p b (t v) -> p b t v", v=VW),
                                         ACT.Copy).then_inc(o_read, 1)
                if not (last and p >= PAIR):
                    if not (first and p < RING):
                        act.wait_ge(pv_done, c - RING + 1)
                    nc.scalar.activation(p_hi[:, p % RING, :], src, ACT.Exp, scale=DH ** -0.5).then_inc(hi_done, 1)

            act.wait_ge(v_lo_done, 2 * NT)
            for p in range(ROT):
                tick(0, p, False, first=True)
            with act.Fori(0, NP - 1) as g:
                for p in range(ROT, ROT + PAIR):
                    tick(g, p, False)
            for p in range(ROT, ROT + PAIR):
                tick(NP - 1, p, True)

            layernorm(3)
            swiglu(1)

        @block.vector
        def _(dve):
            steps = {"n": 0, "g": None, "per": 0}

            def step_wait(k):
                steps["n"] += k
                dve.wait_ge(dve_step, steps["n"] if steps["g"] is None else steps["g"] * steps["per"] + steps["n"])

            def link(ins):
                ins.then_inc(dve_step, 1)
                step_wait(1)

            def cols(b):
                return slice(b * BLK, (b + 1) * BLK)

            def layernorm(k):
                for b in range(NB):
                    dve.wait_ge(squared, NB * k + b + 1)
                    nc.vector.tensor_copy(xnT[:, cols(b)], ps[:, b, :]).then_inc(dve_step, 1)
                dve.wait_ge(rooted, k + 1)
                nc.vector.reciprocal(ln_std, ln_std).then_inc(inverted, 1)
                step_wait(NB)
                for b in range(NB):
                    dve.wait_ge(spread_std, NB * k + b + 1)
                    nc.vector.tensor_tensor(xnT[:, cols(b)], ps[:, 4 + b, :], xnT[:, cols(b)], ALU.mult
                                            ).then_inc(normed, 1)

            def swiglu(f):
                n = NB * FH

                def down(b):
                    dve.wait_ge(down_done, NB * f + b + 1)
                    nc.vector.tensor_tensor(xT[:, cols(b)], ps[:, DOWN_BANK[b], :], xT[:, cols(b)], ALU.add
                                            ).then_inc(x_new, 1)

                for i in range(n):
                    b, j = divmod(i, FH)
                    dve.wait_ge(silu_done, n * f + i + 1)
                    if i >= 3:
                        dve.wait_ge(h_lo_done, n * f + i - 2)
                    nc.vector.tensor_tensor(ff_h[:, i % 3, :], ps[:, 3 + 2 * (i % 3), :], ff_s[:, i % 3, :],
                                            ALU.mult).then_inc(h_done, 1)
                    if j == 2 and b:
                        down(b - 1)
                down(NB - 1)

            nc.vector.memset(eps[:], EPS).then_inc(eps_ready, 1)
            dve.wait_ge(vw_in, 16)
            link(nc.vector.tensor_tensor(wv_sq, wv, wv, ALU.mult))
            nc.vector.tensor_reduce(v_norm, wv_sq, AX, ALU.add).then_inc(v_summed, 1)
            dve.wait_ge(v_rooted, 1)
            link(nc.vector.tensor_scalar(v_norm, v_norm, 1e-30, None, ALU.max))
            link(nc.vector.tensor_scalar(v_pow.bitcast(I32), v_norm.bitcast(I32), 0x7F800000, None,
                                         ALU.bitwise_and))
            nc.vector.tensor_scalar(v_unscale[:], v_pow, 1.0 / V_LIMIT, None, ALU.mult)
            link(nc.vector.reciprocal(v_scale, v_pow))
            link(nc.vector.tensor_scalar(v_scale, v_scale, V_LIMIT, None, ALU.mult))
            nc.vector.tensor_tensor(wv, wv, v_scale.unsqueeze(2).broadcast_to([P, NP, C]), ALU.mult
                                    ).then_inc(wv_scaled, 1)

            dve.wait_ge(a_in, 48)
            for w in (wkv, wkv_b):
                w8 = w.rearrange("p (h d) -> p h d", d=HD)
                link(nc.vector.tensor_reduce(wkv_mean[:, 0:32], w8, AX, ALU.add))
                link(nc.vector.scalar_tensor_tensor(w8, wkv_mean[:, 0:32].unsqueeze(2).broadcast_to([P, 32, HD]),
                                                    -1.0 / HD, w8, ALU.mult, ALU.add))
            for s in range(2):
                for dst, i in ((gamma, s), (beta, 2 + s)):
                    last = nc.vector.tensor_copy(dst[:, s * C:(s + 1) * C].rearrange("p (h d) -> p h d", d=HD),
                                                 gb8[:, i, :].unsqueeze(1).broadcast_to([P, C // HD, HD]))
            last.then_inc(gamma_ready, 1)
            dve.wait_ge(bias_in, 32)
            nc.vector.tensor_tensor(kv_bias.rearrange("p (h e) -> p h e", e=HD),
                                    mask.rearrange("p (h e) -> p h e", e=HD),
                                    kv_bias8.unsqueeze(1).broadcast_to([P, C // HD, HD]), ALU.mult)
            link(nc.vector.tensor_scalar(temp, temp, 1.0 / T, None, ALU.mult))
            layernorm(0)

            def kv_move(u):
                dve.wait_ge(kv_done, u + 1)
                nc.vector.tensor_tensor(kv[:, 4 * u:4 * u + 4, :],
                                        ps[:, 2 * u:2 * u + 2, :].rearrange("p b (t n) -> p (b t) n", n=256),
                                        wkv_b.unsqueeze(1).broadcast_to([P, 4, 256]), ALU.add
                                        ).then_inc(kv_moved, 1)

            def groups(u):
                return kv[:, 4 * u:4 * u + 4, :].rearrange("p t (h d) -> p (t h) d", d=HD)

            def kv_sum(u):
                dve.wait_ge(kv_squared, u + 1)
                nc.vector.tensor_reduce(kv_rstd[:, u, :], kv_sq[:, u % 2, :].rearrange("p (g d) -> p g d", d=HD),
                                        AX, ALU.add).then_inc(kv_summed, 1)

            def kv_norm(u):
                dve.wait_ge(kv_rooted, u + 1)
                link(nc.vector.reciprocal(kv_rstd[:, u, :], kv_rstd[:, u, :]))
                nc.vector.tensor_tensor(groups(u), groups(u),
                                        kv_rstd[:, u, :].unsqueeze(2).broadcast_to([P, 128, HD]), ALU.mult
                                        ).then_inc(kv_scaled, 1)

            kv_move(0)
            kv_move(1)
            kv_sum(0)
            kv_norm(0)
            kv_move(2)
            kv_move(3)
            for u in range(1, 4):
                kv_sum(u)
                kv_norm(u)
            dve.wait_ge(kv_scaled, 4)
            kv_3 = kv[:, 12:16, :]
            link(nc.vector.tensor_tensor(kv_3, kv_3, gamma.unsqueeze(1).broadcast_to([P, 4, 256]), ALU.mult))
            nc.vector.tensor_tensor(kv_3, kv_3, beta.unsqueeze(1).broadcast_to([P, 4, 256]), ALU.add
                                    ).then_inc(last_kv_ready, 1)
            dve.wait_ge(wv_turned, 1)
            wv_ps = ps[:, 5:7, :].rearrange("p b n -> p (b n)")
            link(nc.vector.tensor_copy(wv_hi, wv_ps))
            nc.vector.tensor_tensor(wv_lo, wv_ps, f32(wv_hi), ALU.subtract)
            nc.vector.tensor_scalar(y_bias[:], ps[:, 7, 0:1], out_b[:], None, ALU.add).then_inc(wv_ready, 1)
            dve.wait_ge(kvprod_done, 1)
            link(nc.vector.scalar_tensor_tensor(kv_bd, ps[:, 4, 0:P], temp, mask, ALU.mult, ALU.mult))
            nc.vector.tensor_tensor(kv_bd, kv_bd, kv_bias, ALU.add).then_inc(kv_bd_ready, 1)

            def att_move(b):
                dve.wait_ge(att_done, b + 1)
                nc.vector.tensor_tensor(attT[:, cols(b)], ps[:, b, :], xnT[:, cols(b)], ALU.add).then_inc(att_moved, 1)

            def a_out(b):
                link(nc.vector.tensor_tensor(xT[:, cols(b)], xT[:, cols(b)], xnT[:, cols(b)], ALU.add))
                dve.wait_ge(p2_done, b + 1)
                nc.vector.scalar_tensor_tensor(xT[:, cols(b)], ps[:, b, :], p2b, xT[:, cols(b)], ALU.add, ALU.add
                                               ).then_inc(x_new, 1)

            for b in range(NB):
                att_move(b)
            for b in range(NB):
                a_out(b)

            def split_wkq(i, loaded):
                dve.wait_ge(w_in[i], loaded)
                link(nc.vector.tensor_copy(wkq_hi[:], wkq[:]))
                nc.vector.tensor_tensor(wkq_lo[:], wkq[:], f32(wkq_hi[:]), ALU.subtract
                                        ).then_inc(wkq_ready, 1)

            layernorm(1)
            swiglu(0)
            split_wkq(0, 32)
            layernorm(2)
            def take(job, bank, m, n):
                dve.wait_ge(aux_done, m + 1)
                src = ps[:, bank, :]
                kind, i = job[0], job[1]
                if kind == "proj":
                    b = job[2]
                    link(nc.vector.tensor_scalar(k1[i][:, cols(b)], src, bkq[i][:], None, ALU.add))
                    if b % 2:
                        nc.vector.scalar_tensor_tensor(q2[i][:, cols(b)], src, bkq[i][:], f32(k1[i][:, cols(b)]),
                                                       ALU.add, ALU.subtract).then_inc(aux_used, 1)
                        dve.wait_ge(aux_used, m + 1)
                        dve.sem_inc(kq_split)
                    else:
                        nc.vector.scalar_tensor_tensor(q2[i][:, cols(b)], src, bkq[i][:], f32(k1[i][:, cols(b)]),
                                                       ALU.add, ALU.subtract).then_inc(aux_used, 1)
                elif kind == "max":
                    t, kb = max_operands(job[2])
                    ins = nc.vector.tensor_reduce(maxes[:, t, kb:kb + 1], src, AX, ALU.max).then_inc(aux_used, 1)
                    if job[2] == 4 * NT - 1:
                        dve.wait_ge(aux_used, m + 1)
                        link(nc.vector.tensor_reduce(row_max[:], maxes[:], AX, ALU.max))
                        nc.vector.tensor_scalar(neg_max[:], row_max[:], -1.0, P_SCALE * DH ** 0.5, ALU.mult, ALU.add
                                                ).then_inc(neg_max_ready, 1)
                elif kind == "shift":
                    if not (isinstance(n, int) and n < 0):
                        dve.wait_ge(shift_in, n * 16 + 16)
                    nc.vector.tensor_copy(shift[:], src[0:NT, 0:P]).then_inc(aux_used, 1)
                    dve.wait_ge(aux_used, m + 1)
                    dve.sem_inc(shift_ready)
                elif kind == "turn":
                    nc.vector.tensor_scalar(oT, src, unscale[:], None, ALU.mult).then_inc(aux_used, 1)
                else:
                    nc.vector.tensor_tensor(xT[:, cols(job[1])], src, xT[:, cols(job[1])], ALU.add
                                            ).then_inc(aux_used, 1)

            for b in range(NB):
                take(("proj", 0, b), aux_bank(b, True), b, -1)
            split_wkq(1, 32)
            link(nc.vector.tensor_scalar(xT[:], xT[:], y_bias[:], None, ALU.add))
            for n in range(4 * NT):
                take(("max", 0, n), aux_bank(NB + n, True), NB + n, -1)
            take(("shift", 0), aux_bank(NB + 4 * NT, True), NB + 4 * NT, -1)

            def low(g, p, last):
                c = g * PAIR + p
                dve.wait_ge(hi_done, c + 1)
                if not (isinstance(c, int) and c < RING):
                    dve.wait_ge(pv_done, c - RING + 1)
                nc.vector.tensor_tensor(p_lo[:, p % RING, :], p32[:, p % RING, :], p_hi[:, p % RING, :], ALU.subtract
                                        ).then_inc(lo_dve, 1)

            dve.sem_inc(o_used)

            def o_sum(g, q):
                dve.wait_ge(o_read, g * 8 + q // 8 + 1)
                nc.vector.reciprocal(rden[:].unsqueeze(3), o_raw[:, :, :, DH:DH + 1]).then_inc(dve_step, 1)
                nc.vector.tensor_tensor(o_raw[:, :, :, 0:DH], o_raw[:, :, :, 0:DH], o_raw[:, :, :, DH + 1:VW], ALU.add
                                        ).then_inc(dve_step, 1)
                steps["n"] += 2

            def o_divide(q):
                qb, i = q // 8 % 4, q // HEAD % 2
                dst = o_sb[:, 4 * qb:4 * qb + 4, i * DH:(i + 1) * DH].rearrange("p (b t) d -> p b t d", b=2)
                step_wait(0)
                nc.vector.tensor_tensor(dst, o_raw[:, :, :, 0:DH], rden[:].unsqueeze(3).broadcast_to([P, 2, 2, DH]),
                                        ALU.mult).then_inc(o_used, 1)

            def tick(g, p, last, first=False):
                jobs = first_jobs(p) if first else aux_jobs(p, last)
                done = aux_before(p, last, first)
                q = p - LAG - 1
                ends = q >= 0 and q % 8 == 7 and not (last and q >= PAIR)
                for k in range(3):
                    if k < len(jobs):
                        m = done + k if first else g * AUX_PAIR + done + k
                        take(jobs[k], aux_bank(done + k), m, g * 2 + p // HEAD)
                    if k == 0 and ends:
                        o_sum(g, q)
                    if k == 1 and ends:
                        o_divide(q)
                if p % HEAD == HEAD - 1 and not last:
                    split_wkq(p // HEAD % 2, g * 32 + 64)
                if p and low_on_dve((p - 1) % PAIR, last) and not (last and p - 1 >= PAIR):
                    low(g, p - 1, last)

            for p in range(ROT):
                tick(0, p, False, first=True)
            steps["per"] = 8 + 2 * 8 + 2 + 2
            with dve.Fori(0, NP - 1) as g:
                steps["g"], before = g, steps["n"]
                for p in range(ROT, ROT + PAIR):
                    tick(g, p, False)
                assert steps["n"] - before == steps["per"], steps["n"] - before
            steps["g"], steps["n"] = None, before + (NP - 1) * steps["per"]
            for p in range(ROT, ROT + PAIR):
                tick(NP - 1, p, True)

            layernorm(3)
            swiglu(1)

        @block.gpsimd
        def _(pool):
            def ones_row(i):
                nc.gpsimd.memset(k2[i][0:DH, :].bitcast(F32), 0.0).then_inc(zeros_done, 1)
                pool.wait_ge(zeros_done, 2 - i)
                nc.gpsimd.memset(k2[i][0:1, :].bitcast(F32), 1.0).then_inc(ones_done, 1)

            ones_row(1)

            def w_parts(f):
                pool.wait_ge(ff_in, 32 * (f + 1))
                nc.gpsimd.tensor_scalar(w32, ints, 1.0 / 127.0, None, ALU.mult).then_inc(w32_ready, 1)
                pool.wait_ge(w32_ready, f + 1)
                nc.gpsimd.tensor_copy(w_hi, w32).then_inc(w_hi_ready, 1)
                pool.wait_ge(w_hi_ready, f + 1)
                nc.gpsimd.tensor_tensor(w_lo, w32, f32(w_hi), ALU.subtract).then_inc(w_lo_ready, 1)

            w_parts(0)
            for u in range(3):
                kv_u = kv[:, 4 * u:4 * u + 4, :]
                pool.wait_ge(kv_scaled, u + 1)
                nc.gpsimd.tensor_tensor(kv_u, kv_u, gamma.unsqueeze(1).broadcast_to([P, 4, 256]), ALU.mult
                                        ).then_inc(kv_gamma, 1)
                pool.wait_ge(kv_gamma, u + 1)
                nc.gpsimd.tensor_tensor(kv_u, kv_u, beta.unsqueeze(1).broadcast_to([P, 4, 256]), ALU.add
                                        ).then_inc(kv_ready, 1)
            def xn_low(k):
                for b in range(NB):
                    c = slice(b * BLK, (b + 1) * BLK)
                    pool.wait_ge(xn_hi_done, NB * (k - 1) + b + 1)
                    nc.gpsimd.tensor_tensor(xn_lo[:, c], xnT[:, c], f32(xn_hi[:, c]), ALU.subtract
                                            ).then_inc(xn_lo_done, 1)

            def swiglu(f):
                for i in range(NB * FH):
                    pool.wait_ge(h_hi_done, NB * FH * f + i + 1)
                    hi, lo = h_parts(i)
                    nc.gpsimd.tensor_tensor(lo, ff_h[:, i % 3, :], f32(hi), ALU.subtract).then_inc(h_lo_done, 1)

            xn_low(1)
            swiglu(0)
            xn_low(2)
            ones_row(0)
            pool.wait_ge(x_new, 2 * NB)
            nc.gpsimd.memset(v_all[:, :, :, DH:DH + 1], 1.0).then_inc(ones_done, 1)
            for i in range(2 * NT):
                t, half = divmod(i, 2)
                heads = slice(half * 8, half * 8 + 8)
                pool.wait_ge(v_moved, i + 1)
                nc.gpsimd.tensor_tensor(v_all[:, heads, t, DH + 1:VW],
                                        v32[:, i % 8, :].rearrange("p (h d) -> p h d", d=DH),
                                        v_all[:, heads, t, 0:DH], ALU.subtract).then_inc(v_lo_done, 1)

            def tick(g, p, last, first=False):
                if low_on_dve(p % PAIR, last):
                    return
                c = g * PAIR + p
                pool.wait_ge(hi_done, c + 1)
                if not (first and p < RING):
                    pool.wait_ge(pv_done, c - RING + 1)
                nc.gpsimd.tensor_tensor(p_lo[:, p % RING, :], p32[:, p % RING, :], p_hi[:, p % RING, :], ALU.subtract
                                        ).then_inc(lo_pool, 1)

            for p in range(ROT):
                tick(0, p, False, first=True)
            with pool.Fori(0, NP - 1) as g:
                for p in range(ROT, ROT + PAIR):
                    tick(g, p, False)
            for p in range(ROT, PAIR):
                tick(NP - 1, p, True)
            w_parts(1)
            xn_low(3)
            swiglu(1)


def kernel(**inputs):
    import numpy as np
    import concourse.bacc as bacc
    from concourse.bass_utils import run_bass_kernel_spmd as run

    x = {k.replace("L0_", ""): np.asarray(v) for k, v in inputs.items()}
    C, T, H2, H = 128, x["attn_a_x"].shape[1], 16, 16
    W, bW = x["attn_b_W_w"], x["attn_b_W_b"]
    D = H2 * DH
    by_head = lambda w: w.reshape(H2, DH, *w.shape[1:])
    eye = np.eye(C, dtype=np.float32)
    first_row = np.zeros((C, C), np.float32)
    first_row[::32] = 1.0
    arrays = {
        "xT": x["attn_a_x"][0].T,
        "w_a": np.concatenate([x["attn_a_qkv_w"][C:], x["attn_a_qkv_w"][:C], x["attn_a_p1_w"], x["attn_a_p2_w"]]).T,
        "rows": np.concatenate([x["attn_a_kn_g"], x["attn_a_vn_g"], x["attn_a_kn_b"], x["attn_a_vn_b"],
                                x["attn_a_qkv_b"][C:]]),
        "columns": np.concatenate([
            np.stack([x["attn_a_qkv_b"][:C], x["attn_a_p1_b"], x["attn_a_p2_b"], x["attn_b_out_b"],
                      np.repeat(x["attn_a_temperature"].reshape(-1), C // H)], axis=1),
            x["attn_a_attn_bias"].reshape(C, C // H), bW[2 * D:].reshape(D // C, C).T], axis=1),
        "wkq": np.concatenate([by_head(W[D:2 * D]), by_head(W[0:D])], axis=1).transpose(0, 2, 1),
        "bkq": np.concatenate([by_head(bW[D:2 * D]), by_head(bW[0:D])], axis=1),
        "wv": W[2 * D:], "woT": x["attn_b_out_w"].T,
        "wgu": np.concatenate([x["ffn_w_gate"], x["ffn_w_up"]]).reshape(-1, C, C).transpose(2, 0, 1),
        "wd": x["ffn_w_down"].T,
        "consts": np.stack([eye, eye - np.float32(1.0 / C), np.full((C, C), 1.0 / C, np.float32), first_row], axis=1),
        "mask": np.kron(np.eye(H, dtype=np.float32), np.ones((C // H, C // H), np.float32)),
    }
    nc = bacc.Bacc("TRN2", target_bir_lowering=False, num_devices=1)
    maps, args = {}, {}
    for name, v in arrays.items():
        v = np.ascontiguousarray(v)
        maps[f"in_{name}"] = v
        args[name] = nc.dram_tensor(f"in_{name}", v.shape, mybir.dt.from_np(v.dtype), kind="ExternalInput").ap()
    args["out"] = nc.dram_tensor("out_xT", (C, T), F32, kind="ExternalOutput").ap()
    block_program(nc, args)
    r = run(nc, [maps], core_ids=[0])
    return np.ascontiguousarray(np.asarray(r.results[0]["out_xT"]).T).reshape(1, T, C)
```
